# Optimizing a Trainium2 kernel written in Bass

```python
import numpy as np
import jax
import jax.numpy as jnp

def _softmax(x, axis=-1):
    return jax.nn.softmax(x, axis=axis)

def _gelu(x):
    return jax.nn.gelu(x, approximate=True)

def _silu(x):
    return jax.nn.silu(x)

def _sigmoid(x):
    return jax.nn.sigmoid(x)

def _layernorm(x, axis=-1, eps=1e-05):
    m = jnp.mean(x, axis=axis, keepdims=True)
    v = jnp.var(x, axis=axis, keepdims=True)
    return (x - m) / jnp.sqrt(v + eps)

def _scatter_add(tgt, idx, src, axis=0):
    return tgt.at[idx].add(src)

def _segment_sum(src, seg, n):
    return jax.ops.segment_sum(src, seg, n)
kernel_name = 'mk_cond_resid_d1_seqx_r2_14ba42'

def setup_inputs(seed: int=0):
    np.random.seed(seed)
    _w = jnp.asarray

    def _rec_inputs():
        import jax
        import jax.numpy as jnp
        _rk = jax.random.key(seed)
        x = -0.0002928 + 1 * jax.random.normal(jax.random.fold_in(_rk, 1), (16, 512, 512), jnp.float32)
        _lenS = 512 - jax.random.randint(jax.random.fold_in(_rk, 7), (16,), 0, max(1, 512 // 4) + 1, jnp.int32)
        _lenS2 = 512 - jax.random.randint(jax.random.fold_in(_rk, 8), (16,), 0, max(1, 512 // 4) + 1, jnp.int32)
        cond_64 = -0.0184271 + 1.00439 * jax.random.normal(jax.random.fold_in(_rk, 12), (16, 64), jnp.float32)
        _validS = jnp.arange(512)[None, :] < _lenS[:, None]
        _validS2 = jnp.arange(512)[None, :] < _lenS2[:, None]
        _causal = jnp.tril(jnp.ones((512, 512), dtype=bool))
        mask_BxS_bf1 = jnp.ones((16, 512), dtype=bool)
        return (x, cond_64, mask_BxS_bf1)
    x, cond_64, mask_BxS_bf1 = _rec_inputs()

    def _L0_cond_setup():
        import jax, jax.numpy as jnp
        import numpy as np
        DIM = 512
        HEADS = 16
        DIM_HEAD = 64
        SCALE = 8.0

        def ln(x, g, eps=1e-05):
            mean = x.mean(axis=-1, keepdims=True)
            var = ((x - mean) ** 2).mean(axis=-1, keepdims=True)
            return (x - mean) * jax.lax.rsqrt(var + eps) * g

        def l2norm(t):
            n = jnp.maximum(jnp.linalg.norm(t, axis=-1, keepdims=True), 1e-12)
            return t / n

        def rel_pos_bias(n, w0, b0, g0, w1, b1, g1, w2, b2, dtype):
            pos = jnp.arange(-n + 1, n, dtype=dtype)[:, None]
            h = jax.nn.silu(ln(pos @ w0 + b0, g0))
            h = jax.nn.silu(ln(h @ w1 + b1, g1))
            h = h @ w2 + b2
            i = jnp.arange(n)
            idx = i[:, None] - i[None, :] + n - 1
            bias = h[idx]
            return jnp.transpose(bias, (2, 0, 1))
        key = jax.random.key(seed)
        ks = jax.random.split(key, 16)
        b, n = (2, 1024)
        inner = HEADS * DIM_HEAD
        s = 0.02
        return {'x': jax.random.normal(ks[0], (b, n, DIM), jnp.float32), 'mask': jnp.ones((b, n), dtype=bool), 'g_norm': jnp.ones((DIM,), jnp.float32), 'Wq': jax.random.normal(ks[1], (DIM, inner), jnp.float32) * s, 'Wkv': jax.random.normal(ks[2], (DIM, 2 * DIM_HEAD), jnp.float32) * s, 'q_scale': jnp.ones((DIM_HEAD,), jnp.float32), 'k_scale': jnp.ones((DIM_HEAD,), jnp.float32), 'null_kv': jax.random.normal(ks[3], (2, DIM_HEAD), jnp.float32), 'null_attn_bias': jax.random.normal(ks[4], (HEADS,), jnp.float32), 'w0': jax.random.normal(ks[5], (1, DIM), jnp.float32) * s, 'b0': jnp.zeros((DIM,), jnp.float32), 'g0': jnp.ones((DIM,), jnp.float32), 'w1': jax.random.normal(ks[6], (DIM, DIM), jnp.float32) * s, 'b1': jnp.zeros((DIM,), jnp.float32), 'g1': jnp.ones((DIM,), jnp.float32), 'w2': jax.random.normal(ks[7], (DIM, HEADS), jnp.float32) * s, 'b2': jnp.zeros((HEADS,), jnp.float32), 'Wout': jax.random.normal(ks[8], (inner, DIM), jnp.float32) * s, 'g_out': jnp.ones((DIM,), jnp.float32)}
    _L0_cond_all = _L0_cond_setup()
    _L0_cond_in = {k: v for k, v in _L0_cond_all.items() if k in ('g_norm', 'Wq', 'Wkv', 'q_scale', 'k_scale', 'null_attn_bias', 'w0', 'b0', 'g0', 'w1', 'b1', 'g1', 'w2', 'b2', 'Wout', 'g_out')}
    del _L0_cond_all
    return {'x': x, 'cond_64': cond_64, 'mask_BxS_bf1': mask_BxS_bf1, 'L0_cond_g_norm': _L0_cond_in['g_norm'], 'L0_cond_Wq': _L0_cond_in['Wq'], 'L0_cond_Wkv': _L0_cond_in['Wkv'], 'L0_cond_q_scale': _L0_cond_in['q_scale'], 'L0_cond_k_scale': _L0_cond_in['k_scale'], 'L0_cond_null_attn_bias': _L0_cond_in['null_attn_bias'], 'L0_cond_w0': _L0_cond_in['w0'], 'L0_cond_b0': _L0_cond_in['b0'], 'L0_cond_g0': _L0_cond_in['g0'], 'L0_cond_w1': _L0_cond_in['w1'], 'L0_cond_b1': _L0_cond_in['b1'], 'L0_cond_g1': _L0_cond_in['g1'], 'L0_cond_w2': _L0_cond_in['w2'], 'L0_cond_b2': _L0_cond_in['b2'], 'L0_cond_Wout': _L0_cond_in['Wout'], 'L0_cond_g_out': _L0_cond_in['g_out']}

def reference(x, cond_64, mask_BxS_bf1, L0_cond_g_norm, L0_cond_Wq, L0_cond_Wkv, L0_cond_q_scale, L0_cond_k_scale, L0_cond_null_attn_bias, L0_cond_w0, L0_cond_b0, L0_cond_g0, L0_cond_w1, L0_cond_b1, L0_cond_g1, L0_cond_w2, L0_cond_b2, L0_cond_Wout, L0_cond_g_out):
    import jax
    import jax.numpy as jnp

    def _L0_cond_ref(x, mask, g_norm, Wq, Wkv, q_scale, k_scale, null_kv, null_attn_bias, w0, b0, g0, w1, b1, g1, w2, b2, Wout, g_out):
        import jax, jax.numpy as jnp
        import numpy as np
        DIM = 512
        HEADS = 16
        DIM_HEAD = 64
        SCALE = 8.0

        def ln(x, g, eps=1e-05):
            mean = x.mean(axis=-1, keepdims=True)
            var = ((x - mean) ** 2).mean(axis=-1, keepdims=True)
            return (x - mean) * jax.lax.rsqrt(var + eps) * g

        def l2norm(t):
            n = jnp.maximum(jnp.linalg.norm(t, axis=-1, keepdims=True), 1e-12)
            return t / n

        def rel_pos_bias(n, w0, b0, g0, w1, b1, g1, w2, b2, dtype):
            pos = jnp.arange(-n + 1, n, dtype=dtype)[:, None]
            h = jax.nn.silu(ln(pos @ w0 + b0, g0))
            h = jax.nn.silu(ln(h @ w1 + b1, g1))
            h = h @ w2 + b2
            i = jnp.arange(n)
            idx = i[:, None] - i[None, :] + n - 1
            bias = h[idx]
            return jnp.transpose(bias, (2, 0, 1))
        b, n, _ = x.shape
        xn = ln(x, g_norm)
        q = (xn @ Wq).reshape(b, n, HEADS, DIM_HEAD).transpose(0, 2, 1, 3)
        kv = xn @ Wkv
        k, v = (kv[..., :DIM_HEAD], kv[..., DIM_HEAD:])
        nk = jnp.broadcast_to(null_kv[0], (b, 1, DIM_HEAD))
        nv = jnp.broadcast_to(null_kv[1], (b, 1, DIM_HEAD))
        k = jnp.concatenate([nk, k], axis=1)
        v = jnp.concatenate([nv, v], axis=1)
        q = l2norm(q) * q_scale
        k = l2norm(k) * k_scale
        sim = jnp.einsum('bhid,bjd->bhij', q, k) * SCALE
        bias = rel_pos_bias(n, w0, b0, g0, w1, b1, g1, w2, b2, q.dtype)
        null_bias = jnp.broadcast_to(null_attn_bias[:, None, None], (HEADS, n, 1))
        attn_bias = jnp.concatenate([null_bias, bias], axis=-1)
        sim = sim + attn_bias
        neg = -jnp.finfo(sim.dtype).max
        causal = jnp.triu(jnp.ones((n, n + 1), dtype=bool), k=2)
        sim = jnp.where(causal, neg, sim)
        m = jnp.pad(mask, ((0, 0), (1, 0)), constant_values=True)[:, None, None, :]
        sim = jnp.where(m, sim, neg)
        attn = jax.nn.softmax(sim, axis=-1)
        out = jnp.einsum('bhij,bjd->bhid', attn, v)
        out = out.transpose(0, 2, 1, 3).reshape(b, n, HEADS * DIM_HEAD)
        return ln(out @ Wout, g_out)
    x = x + _L0_cond_ref(x, mask_BxS_bf1, L0_cond_g_norm, L0_cond_Wq, L0_cond_Wkv, L0_cond_q_scale, L0_cond_k_scale, cond_64, L0_cond_null_attn_bias, L0_cond_w0, L0_cond_b0, L0_cond_g0, L0_cond_w1, L0_cond_b1, L0_cond_g1, L0_cond_w2, L0_cond_b2, L0_cond_Wout, L0_cond_g_out)
    return x

_drawn_inputs = setup_inputs


def setup_inputs(seed=0):
    import zlib

    import numpy as np

    out = dict(_drawn_inputs(seed))
    spreads = {'L0_cond_g_norm': (1.0, 0.2),
     'L0_cond_q_scale': (1.0, 0.2),
     'L0_cond_k_scale': (1.0, 0.2),
     'L0_cond_b0': (0.0, 0.285),
     'L0_cond_g0': (1.0, 0.6),
     'L0_cond_b1': (0.0, 0.412),
     'L0_cond_g1': (1.0, 0.6),
     'L0_cond_b2': (0.0, 0.8),
     'L0_cond_g_out': (1.0, 0.2)}
    factors = {}
    for name, (base, spread) in spreads.items():
        noise = np.random.default_rng([zlib.crc32(name.encode()), seed]).standard_normal(out[name].shape)
        drawn = base * np.exp(spread * noise) if base else spread * noise
        out[name] = jnp.asarray(drawn.astype(out[name].dtype))
    for name, factor in factors.items():
        out[name] = (out[name] * factor).astype(out[name].dtype)
    return out
```

```python
import concourse.bass as bass
from concourse import mybir
from contextlib import ExitStack


def cond_attention_kernel(nc, x, cond, mask, g_norm, wq, wkv, q_scale, k_scale, null_bias,
                          w0, b0, g0, w1, b1, g1, w2, b2, wout, g_out, table_dram, out):
    f32, f32r, bf16, u8 = mybir.dt.float32, mybir.dt.float32r, mybir.dt.bfloat16, mybir.dt.uint8
    ALU = mybir.AluOpType
    ACT = mybir.ActivationFunctionType
    AX = mybir.AxisListType

    P = 128
    B, S, D = x.shape
    NT = S // P
    TILES = B * NT
    DC = D // P
    DH = q_scale.shape[0]
    H = null_bias.shape[0]
    INNER = H * DH
    PAIRS = H // 2
    HALF = INNER // 2
    KVN = 2 * DH + H
    QUAD = 4
    TW = S + P
    SCALE, LN_EPS, L2_EPS = 8.0, 1e-5, 1e-12
    MASKED = -1.5e38
    LAG_T, LAG_V = 8, 10
    TR, PR, SR = 16, 4, 3

    X_AT, KV_AT, Q0_AT, Q1_AT, QT0_AT, P0T_AT, QT1_AT, OUT_AT, KT_AT = 0, 2, 4, 5, 10, 11, 12, 13, 14

    x_v = x.rearrange("b (t p) d -> b t p d", p=P)
    out_v = out.rearrange("b (t p) d -> b t p d", p=P)

    ctx = ExitStack()
    with ctx:
        def sb(name, shape, dt=f32):
            return ctx.enter_context(nc.sbuf_tensor(name, shape, dt))

        def sem(name):
            return ctx.enter_context(nc.semaphore(name))

        wq_h, wq_l = sb("wq_h", [P, DC, INNER], f32r), sb("wq_l", [P, DC, INNER], f32r)
        wk_h, wk_l = sb("wk_h", [P, DC, KVN], f32r), sb("wk_l", [P, DC, KVN], f32r)
        wo_h, wo_l = sb("wo_h", [P, PAIRS, D], f32r), sb("wo_l", [P, PAIRS, D], f32r)
        bias = sb("bias", [P, H, S])
        null_w = sb("null_w", [H, D])
        ident, flip = sb("ident", [P, P]), sb("flip", [P, P])
        g_out_b = sb("g_out_b", [P, D])
        qk_scale = sb("qk_scale", [P, DH])
        neg_null_bias = sb("neg_null_bias", [P, H])
        neg_half = sb("neg_half", [P, H + 1])
        ones64 = sb("ones64", [P, P], bf16)
        x_in = sb("x_in", [P, 4, D])
        x_norm = sb("x_norm", [P, D])
        xT_h, xT_l = sb("xT_h", [P, DC, P], f32r), sb("xT_l", [P, DC, P], f32r)
        kv = sb("kv", [P, 2, KVN])
        squares = sb("squares", [P, 2, HALF])
        norm2 = sb("norm2", [P, 2, H + 1])
        norm2c = sb("norm2c", [P, 2, H + 1])
        rnorm = sb("rnorm", [P, 2, H + 1])
        q_norm = sb("q_norm", [P, INNER])
        k_norm = sb("k_norm", [P, 2, DH])
        null_s = sb("null_s", [P, H])
        neg_null_s = sb("neg_null_s", [P, 2, H])
        qT_h, qT_l = sb("qT_h", [P, 2, PAIRS, P], f32r), sb("qT_l", [P, 2, PAIRS, P], f32r)
        kT_h, kT_l = sb("kT_h", [P, S], f32r), sb("kT_l", [P, S], f32r)
        v = sb("v", [P, NT, DH])
        mask_u8, mask_b = sb("mask_u8", [P, S], u8), sb("mask_b", [P, S], bf16)
        probs = sb("probs", [P, TR + PR, S])
        neg_max, sums, null_e = sb("neg_max", [P, 2, H]), sb("sums", [P, 2, H]), sb("null_e", [P, 2, H])
        null_d, den, rden = sb("null_d", [P, 2, H]), sb("den", [P, 2, H]), sb("rden", [P, 2, H])
        null_p = sb("null_p", [P, 2, H])
        null_pT = sb("null_pT", [H, P])
        oT_h, oT_l = sb("oT_h", [P, PAIRS, P], f32r), sb("oT_l", [P, PAIRS, P], f32r)
        y = sb("y", [P, 2, D])
        x_st, x_mv, x_ve, x_rs = sb("x_st", [P, 6]), sb("x_mv", [P, 2]), sb("x_ve", [P, 1]), sb("x_rs", [P, 1])
        o_st, o_mv, o_ve, o_rs = sb("o_st", [P, 6]), sb("o_mv", [P, 2]), sb("o_ve", [P, 1]), sb("o_rs", [P, 1])
        g_norm_c, b2_c, v_null = sb("g_norm_c", [P, DC]), sb("b2_c", [H, 1]), sb("v_null", [P, 1])
        w2_sb, pos = sb("w2_sb", [P, DC, H]), sb("pos", [P, NT])
        s_st, s_mv, s_ve, s_rs = sb("s_st", [P, NT, 6]), sb("s_mv", [P, NT, 2]), sb("s_ve", [P, NT]), sb("s_rs", [P, NT])

        psum = [ctx.enter_context(nc.psum_tensor(f"bank{i}", [P, 512], f32)) for i in range(8)]
        score_bank, pT_bank, o_bank, m0, m1 = psum[0:SR], psum[SR:SR + 2], psum[5], psum[6], psum[7]

        x_loaded = [sem(f"x_loaded{i}") for i in range(4)]
        y_stored = [sem(f"y_stored{i}") for i in range(2)]
        mask_loaded = sem("mask_loaded")
        xT_made, kv_made, q_made, qT_made = sem("xT_made"), sem("kv_made"), sem("q_made"), sem("qT_made")
        kT_made, null_pT_made, out_made = sem("kT_made"), sem("null_pT_made"), sem("out_made")
        scores_made, pT_made, pv_made = sem("scores_made"), sem("pT_made"), sem("pv_made")
        xTh_ready, kv_copied, k_sq, q_sq = sem("xTh_ready"), sem("kv_copied"), sem("k_sq"), sem("q_sq")
        qTh_ready, kTh_ready, null_pT_ready = sem("qTh_ready"), sem("kTh_ready"), sem("null_pT_ready")
        exp_done, null_e_done, pT_even, oTh_ready = sem("exp_done"), sem("null_e_done"), sem("pT_even"), sem("oTh_ready")
        x_st_done, x_mv_done, x_ve_done, x_norm_done = sem("x_st_done"), sem("x_mv_done"), sem("x_ve_done"), sem("x_norm_done")
        xTl_ready, norm2_done, norm2c_done, q_norm_done = sem("xTl_ready"), sem("norm2_done"), sem("norm2c_done"), sem("q_norm_done")
        k_norm_done, qTl_ready, kTl_ready, mask_ready = sem("k_norm_done"), sem("qTl_ready"), sem("kTl_ready"), sem("mask_ready")
        biased, null_d_done, den_done, rden_done = sem("biased"), sem("null_d_done"), sem("den_done"), sem("rden_done")
        pT_odd, oTl_ready = sem("pT_odd"), sem("oTl_ready")
        o_st_done, o_mv_done, o_ve_done, z_done, y_done = sem("o_st_done"), sem("o_mv_done"), sem("o_ve_done"), sem("z_done"), sem("y_done")
        x_rs_done, rnorm_done, null_s_done, neg_null_s_done = sem("x_rs_done"), sem("rnorm_done"), sem("null_s_done"), sem("neg_null_s_done")
        scaled, null_p_done, v_copied, o_rs_done = sem("scaled"), sem("null_p_done"), sem("v_copied"), sem("o_rs_done")
        passed = sem("passed")
        dma_wq, dma_wout, dma_wkv, dma_small, dma_mlp = sem("dma_wq"), sem("dma_wout"), sem("dma_wkv"), sem("dma_small"), sem("dma_mlp")
        table_stored, table_back = sem("table_stored"), [sem(f"table_back{i}") for i in range(4)]
        zeroed, table_tail, ident_made, pos_made = sem("zeroed"), sem("table_tail"), sem("ident_made"), sem("pos_made")
        k_null_ve, k_null_rs, v_null_placed = sem("k_null_ve"), sem("k_null_rs"), sem("v_null_placed")
        mlp_link, mlp_ve, mlp_rs, mlp_affine = sem("mlp_link"), sem("mlp_ve"), sem("mlp_rs"), sem("mlp_affine")
        mlp_tanh, mlp_silu, hT_made, hT_ready, h2_made = sem("mlp_tanh"), sem("mlp_silu"), sem("hT_made"), sem("hT_ready"), sem("h2_made")
        wqh_made, wkh_made, woh_made, wk_null = sem("wqh_made"), sem("wkh_made"), sem("woh_made"), sem("wk_null")
        dve_staged = sem("dve_staged")
        null_w_made, null_w_ready = sem("null_w_made"), sem("null_w_ready")
        table_made, table_ready = sem("table_made"), sem("table_ready")
        flipped, bias_even, bias_odd = sem("flipped"), sem("bias_even"), sem("bias_odd")

        v_null_sel = q_norm[:, 0:PAIRS * H].rearrange("p (a h) -> p a h", a=PAIRS)
        k_null, k_null_sq = q_norm[:, 512:512 + DH], q_norm[:, 576:576 + DH]
        qk_tmp = q_norm[:, 640:640 + 2 * DH].rearrange("p (a d) -> p a d", a=2)
        table = squares[0:H].rearrange("p a n -> p (a n)")[:, 0:TW]
        wkv_f = y[:].rearrange("p a n -> p (a n)")[:, 0:DC * KVN].rearrange("p (c n) -> p c n", c=DC)
        wq_stage = probs[:, 0:8, :].rearrange("p (c a) n -> p c (a n)", c=DC)
        wout_stage = probs[:, 8:16, :]
        hT = probs[:, 16:20, :]
        mlp_h, mlp_w1, mlp_w0 = bias[:, 0:4, :], bias[:, 4:8, :], bias[:, 8, :]
        mlp_b, mlp_g = (bias[:, 9, :], bias[:, 11, :]), (bias[:, 10, :], bias[:, 12, :])
        tanh = [bias[:, 13 + i, :] for i in range(3)]

        block = ctx.enter_context(nc.Block())

        def need(eng, semaphore, value):
            if not isinstance(value, int) or value > 0:
                eng.wait_ge(semaphore, value)

        def need_apart(eng, semaphore, value):
            need(eng, semaphore, value)
            if not isinstance(value, int):
                eng.sem_inc(passed, 1)

        def tile_of(b, j):
            return b * NT + j

        def real(b, j, offset=0):
            return not isinstance(b, int) or 0 <= b * NT + j + offset < TILES

        def where(b, j, offset):
            return b + (j + offset) // NT, (j + offset) % NT

        def run(eng, step):
            for t in range(-2, NT):
                for h in range(H):
                    step(t // NT, t % NT, h)
            with eng.Fori(1, B - 1) as b:
                for j in range(NT):
                    for h in range(H):
                        step(b, j, h)
            for t in range((B - 1) * NT, B * NT + 1):
                for h in range(H):
                    step(t // NT, t % NT, h)

        def ring_before(s, ring):
            return s - ring if s >= ring else max(o for o in range(NT * H) if o % ring == s % ring) - NT * H

        def head_at(b, j, h, lag):
            off, hh = (h - lag) // H, (h - lag) % H
            bb, jj = where(b, j, off)
            return bb, jj, hh, real(b, j, off)

        def lo_half(eng, dst, src, hi):
            return eng.tensor_tensor(dst, src, hi.bitcast(f32), ALU.subtract)

        @block.sync
        def _(sp):
            def bcast(ap, n=P):
                return ap.partition_broadcast(n)

            sp.dma_start(g_norm_c[:], g_norm.rearrange("(c p) -> p c", p=P), allow_slow_non_contiguous=True).then_inc(dma_small, 16)
            sp.dma_start(k_null, bcast(cond[0, :])).then_inc(dma_small, 16)
            sp.dma_start(qk_tmp[:, 0, :], bcast(q_scale)).then_inc(dma_small, 16)
            sp.dma_start(qk_tmp[:, 1, :], bcast(k_scale)).then_inc(dma_small, 16)
            for i in range(2):
                sp.dma_start(v_null[i * DH:(i + 1) * DH, :], cond[1, :].rearrange("(p a) -> p a", a=1)).then_inc(dma_small, 16)
            sp.dma_start(neg_null_bias[:], bcast(null_bias)).then_inc(dma_small, 16)
            sp.dma_start(b2_c[:], b2.rearrange("(p a) -> p a", a=1)).then_inc(dma_small, 16)
            sp.dma_start(g_out_b[:], bcast(g_out)).then_inc(dma_small, 16)
            for place, w in ((mlp_w0, w0[0, :]), (mlp_b[0], b0), (mlp_g[0], g0), (mlp_b[1], b1), (mlp_g[1], g1)):
                sp.dma_start(place, bcast(w)).then_inc(dma_mlp, 16)
            sp.dma_start(mlp_w1, w1.rearrange("(c p) n -> p c n", p=P)).then_inc(dma_mlp, 16)
            sp.dma_start(w2_sb[:], w2.rearrange("(c p) n -> p c n", p=P)).then_inc(dma_mlp, 16)
            sp.dma_start(wq_stage, wq.rearrange("(c p) n -> p c n", p=P)).then_inc(dma_wq, 16)
            sp.dma_start(wkv_f[:, :, 0:2 * DH], wkv.rearrange("(c p) n -> p c n", p=P)).then_inc(dma_wkv, 16)
            sp.dma_start(wout_stage, wout.rearrange("(c p) n -> p c n", p=P)).then_inc(dma_wout, 16)
            sp.dma_start(x_in[:, 0, :], x_v[0, 0]).then_inc(x_loaded[0], 16)
            sp.wait_ge(table_ready, 1)
            sp.wait_ge(table_tail, 1)
            sp.dma_start(table_dram, table).then_inc(table_stored, 16)
            sp.wait_ge(table_stored, 16)
            sp.wait_ge(dve_staged, 3)
            sp.wait_ge(wqh_made, DC)
            sp.wait_ge(woh_made, 1)
            sp.wait_ge(null_w_made, 1)
            for i in range(4):
                hs = H // 4
                src = bass.AP(table_dram.tensor, i * hs * TW, [[1, P], [TW, hs], [1, S]])
                sp.dma_start(probs[:, i * hs:(i + 1) * hs, :], src).then_inc(table_back[i], 16)

            def step(b, j, h):
                if h == 0 and real(b, j, 3):
                    bb, jj = where(b, j, 3)
                    need_apart(sp, y_done, tile_of(bb, jj) - 4 + 1)
                    sp.dma_start(x_in[:, jj, :], x_v[bb, jj]).then_inc(x_loaded[jj], 16)
                if h == 0 and j == 2 and real(b, j, 2):
                    need_apart(sp, mask_ready, b + 1)
                    sp.dma_start(mask_u8[:], bcast(mask[b + 1, :])).then_inc(mask_loaded, 16)
                if h == H - 1 and real(b, j, -1):
                    bb, jj = where(b, j, -1)
                    need_apart(sp, y_done, tile_of(bb, jj) + 1)
                    sp.dma_start(out_v[bb, jj], y[:, jj % 2, :]).then_inc(y_stored[jj % 2], 16)

            run(sp, step)
            for i in range(2):
                sp.wait_ge(y_stored[i], 16 * TILES // 2)

        @block.tensor
        def _(pe):
            pe.wait_ge(v_null_placed, 1)
            pe.wait_ge(dma_wout, 16)
            for p in range(PAIRS):
                last = nc.tensor.matmul(psum[7][0:H, :], v_null_sel[:, p, :], wout_stage[:, p, :], start=(p == 0), stop=(p == PAIRS - 1))
            last.then_inc(null_w_made, 1)
            pe.wait_ge(ident_made, 2)
            pe.wait_ge(dma_mlp, 7 * 16)
            for layer in range(2):
                pe.wait_ge(mlp_silu, NT * (layer + 1))
                if layer == 1:
                    pe.wait_ge(null_w_ready, 1)
                for c in range(DC):
                    for t in range(NT):
                        last = nc.tensor.transpose(psum[4 * layer + c][:, t * P:(t + 1) * P], mlp_h[:, t, c * P:(c + 1) * P], ident[:])
                    last.then_inc(hT_made, 1)
                pe.wait_ge(hT_ready, DC * (layer + 1))
                if layer == 0:
                    for t in range(NT):
                        for c in range(DC):
                            last = nc.tensor.matmul(psum[t][:], hT[:, c, t * P:(t + 1) * P], mlp_w1[:, c, :], start=(c == 0), stop=(c == DC - 1))
                        last.then_inc(h2_made, 1)
            for c in range(DC):
                last = nc.tensor.matmul(psum[0][0:H, :], w2_sb[:, c, :], hT[:, c, :], start=(c == 0), stop=(c == DC - 1))
            last.then_inc(table_made, 1)
            pe.wait_ge(table_ready, 1)
            for h in range(H):
                if h % 4 == 0:
                    pe.wait_ge(table_back[h // 4], 16)
                if h >= 8:
                    pe.wait_ge(bias_odd if h % 2 else bias_even, (h - 8) // 2 + 1)
                nc.tensor.matmul(psum[h % 8][:], flip[:], probs[:, h, :], start=True, stop=True).then_inc(flipped, 1)
            pe.wait_ge(bias_even, H // 2)
            pe.wait_ge(bias_odd, H // 2)
            pe.wait_ge(dve_staged, 3)


            def three(dst, a_h, a_l, b_h, b_l, first, last):
                nc.tensor.matmul(dst, a_h, b_h, start=first, stop=False)
                nc.tensor.matmul(dst, a_h, b_l, start=False, stop=False)
                return nc.tensor.matmul(dst, a_l, b_h, start=False, stop=last)

            def piece(b, j, h):
                up, (ub, uj) = real(b, j, 1), where(b, j, 1)
                U = tile_of(ub, uj)
                down, (ob, oj) = real(b, j, -1), where(b, j, -1)
                O = tile_of(ob, oj)
                if h == X_AT and up:
                    need(pe, x_norm_done, U + 1)
                    need(pe, kTl_ready, U)
                    for c in range(DC):
                        last = nc.tensor.transpose(m0[:, c * P:(c + 1) * P], x_norm[:, c * P:(c + 1) * P], ident[:])
                    last.then_inc(xT_made, 1)
                if h == KV_AT and up:
                    need(pe, xTl_ready, U + 1)
                    need(pe, z_done, U - 2)
                    for c in range(DC):
                        last = three(m1[:, 0:KVN], xT_h[:, c, :], xT_l[:, c, :], wk_h[:, c, :], wk_l[:, c, :], c == 0, c == DC - 1)
                    last.then_inc(kv_made, 1)
                for half, at, bank in ((0, Q0_AT, m0), (1, Q1_AT, m1)):
                    if h == at and up:
                        if half:
                            need(pe, kv_copied, U + 1)
                        cols = slice(half * HALF, (half + 1) * HALF)
                        for c in range(DC):
                            last = three(bank[:], xT_h[:, c, :], xT_l[:, c, :], wq_h[:, c, cols], wq_l[:, c, cols], c == 0, c == DC - 1)
                        last.then_inc(q_made, 1)
                for half, at in ((0, QT0_AT), (1, QT1_AT)):
                    if h == at and up:
                        need(pe, q_norm_done, 2 * U + 2)
                        if half:
                            need(pe, qTl_ready, 2 * U + 1)
                        for i in range(PAIRS // 2):
                            c = half * HALF + i * P
                            last = nc.tensor.transpose(m0[:, i * P:(i + 1) * P], q_norm[:, c:c + P], ident[:])
                        last.then_inc(qT_made, 1)
                if h == KT_AT and up:
                    need(pe, k_norm_done, U + 1)
                    need(pe, qTl_ready, 2 * U + 2)
                    nc.tensor.transpose(m0[:, 0:P], k_norm[:].rearrange("p a d -> p (a d)"), ident[:]).then_inc(kT_made, 1)
                if h == P0T_AT and down:
                    need(pe, null_p_done, 4 * O + 4)
                    if up:
                        need(pe, q_norm_done, 2 * U + 2)
                    nc.tensor.transpose(m1[0:H, 0:P], null_p[:, oj % 2, :], ident[:]).then_inc(null_pT_made, 1)
                if h == OUT_AT and down:
                    need(pe, null_pT_ready, O + 1)
                    need(pe, oTl_ready, 2 * O + 2)
                    for p in range(PAIRS):
                        three(m1[:], oT_h[:, p, :], oT_l[:, p, :], wo_h[:, p, :], wo_l[:, p, :], p == 0, False)
                    nc.tensor.matmul(m1[:], null_pT[:], null_w[:], start=False, stop=True).then_inc(out_made, 1)

            def step(b, j, h):
                bb, jj, hh, there = head_at(b, j, h, LAG_T)
                if there:
                    s = tile_of(bb, jj) * H + hh
                    need(pe, scaled, tile_of(bb, jj) * PAIRS + hh // 2 + 1)
                    need(pe, pT_odd if hh % 2 else pT_even, tile_of(bb, jj) * PAIRS + hh // 2)
                    for k in range(jj + 1):
                        last = nc.tensor.transpose(pT_bank[hh % 2][:, k * P:(k + 1) * P], probs[:, hh, k * P:(k + 1) * P], ident[:])
                    last.then_inc(pT_made, 1)
                bb, jj, hh, there = head_at(b, j, h, LAG_V)
                if there and hh % 2:
                    T, m = tile_of(bb, jj), hh // 2
                    need(pe, pT_even, T * PAIRS + m + 1)
                    need(pe, pT_odd, T * PAIRS + m + 1)
                    if m == 0:
                        need(pe, v_copied, T + 1)
                    if m % 4 == 0:
                        need(pe, oTl_ready, 2 * T + m // 4)
                    c = (m % 4) * P
                    for k in range(jj + 1):
                        for i in range(2):
                            last = nc.tensor.matmul(o_bank[i * DH:(i + 1) * DH, c:c + P], v[:, k, :],
                                                    probs[:, TR + (hh - 1 + i) % PR, k * P:(k + 1) * P],
                                                    start=(k == 0), stop=(k == jj))
                    last.then_inc(pv_made, 1)
                piece(b, j, h)
                if real(b, j):
                    T, n = tile_of(b, j), (j + 1) * P
                    if h == 0:
                        need(pe, kTl_ready, T + 1)
                        need(pe, mask_ready, b + 1)
                    if h % 8 == 0:
                        need(pe, qTl_ready, 2 * T + h // 8 + 1)
                    before = ring_before(j * H + h, SR)
                    need(pe, biased, b * NT * H + before + 1)
                    bank = score_bank[(j * H + h) % SR]
                    rows = slice((h % 2) * DH, (h % 2 + 1) * DH)
                    nc.tensor.matmul(bank[:, 0:n], ones64[rows, :], mask_b[rows, 0:n], start=True, stop=False)
                    three(bank[:, 0:n], qT_h[rows, j % 2, h // 2, :], qT_l[rows, j % 2, h // 2, :],
                          kT_h[rows, 0:n], kT_l[rows, 0:n], False, True).then_inc(scores_made, 1)

            run(pe, step)

        @block.scalar
        def _(act):
            for t in range(NT):
                act.wait_ge(mlp_affine, t + 1)
                if t == 3:
                    act.wait_ge(mlp_silu, 1)
                nc.scalar.activation(tanh[t % 3], mlp_h[:, t, :], ACT.Tanh, scale=0.5).then_inc(mlp_tanh, 1)
            act.wait_ge(dma_wq, 16)
            act.wait_ge(dma_small, 9 * 16)
            for c in range(DC):
                nc.scalar.activation(wq_h[:, c, :], wq_stage[:, c, :], ACT.Copy, scale=g_norm_c[:, c:c + 1]).then_inc(wqh_made, 1)
            for layer in range(2):
                for c in range(DC):
                    act.wait_ge(hT_made, DC * layer + c + 1)
                    if layer == 1 and c == 0:
                        act.wait_ge(h2_made, NT)
                    nc.scalar.activation(hT[:, c, :], psum[4 * layer + c][:], ACT.Copy, scale=0.5).then_inc(hT_ready, 1)
                if layer == 0:
                    act.wait_ge(dma_wout, 16)
                    nc.scalar.activation(wo_h[:].rearrange("p c n -> p (c n)"), wout_stage.rearrange("p c n -> p (c n)"), ACT.Copy).then_inc(woh_made, 1)
                    act.wait_ge(null_w_made, 1)
                    nc.scalar.activation(null_w[:], psum[7][0:H, :], ACT.Copy).then_inc(null_w_ready, 1)
                    act.wait_ge(wk_null, DC)
                    act.wait_ge(dma_wkv, 16)
                    for c in range(DC):
                        nc.scalar.activation(wk_h[:, c, :], wkv_f[:, c, :], ACT.Copy, scale=g_norm_c[:, c:c + 1]).then_inc(wkh_made, 1)
                    for t in range(NT):
                        act.wait_ge(mlp_affine, NT + t + 1)
                        act.wait_ge(mlp_silu, t + (2 if t < 3 else NT + 1 - 3))
                        nc.scalar.activation(tanh[(t + 1) % 3], mlp_h[:, t, :], ACT.Tanh, scale=0.5).then_inc(mlp_tanh, 1)
            for h in range(0, H, 2):
                act.wait_ge(flipped, h + 1)
                nc.scalar.activation(bias[:, h, :], psum[h % 8][:], ACT.Copy).then_inc(bias_even, 1)


            def step(b, j, h):
                bb, jj, hh, there = head_at(b, j, h, LAG_T)
                if there and hh % 2 == 0:
                    T = tile_of(bb, jj)
                    need(act, pT_made, T * H + hh + 1)
                    need(act, pv_made, T * PAIRS + hh // 2 - PR // 2 + 1)
                    n = (jj + 1) * P
                    nc.scalar.activation(probs[:, TR + hh % PR, 0:n], pT_bank[0][:, 0:n], ACT.Copy).then_inc(pT_even, 1)
                up, (ub, uj) = real(b, j, 1), where(b, j, 1)
                U = tile_of(ub, uj)
                if up and h == X_AT + 1:
                    need(act, xT_made, U + 1)
                    nc.scalar.activation(xT_h[:].rearrange("p c n -> p (c n)"), m0[:], ACT.Copy).then_inc(xTh_ready, 1)
                if up and h == KV_AT + 1:
                    need(act, kv_made, U + 1)
                    need(act, v_copied, U - 1)
                    nc.scalar.activation(kv[:, uj % 2, :], m1[:, 0:KVN], ACT.Copy).then_inc(kv_copied, 1)
                    need(act, kv_copied, U + 1)
                    nc.scalar.activation(squares[:, 0, 0:DH], kv[:, uj % 2, 0:DH], ACT.Square,
                                         accum_out=norm2[:, uj % 2, H:H + 1]).then_inc(k_sq, 1)
                for half, at, bank in ((0, Q0_AT, m0), (1, Q1_AT, m1)):
                    if up and h == at + 1:
                        need(act, q_made, 2 * U + half + 1)
                        need(act, norm2_done, 2 * U + half - 1)
                        if half == 0:
                            need(act, k_sq, U + 1)
                        nc.scalar.activation(squares[:, half, :], bank[:], ACT.Square).then_inc(q_sq, 1)
                for half, at in ((0, QT0_AT), (1, QT1_AT)):
                    if up and h == at + 1:
                        need(act, qT_made, 2 * U + half + 1)
                        need(act, scores_made, (U - 1) * H)
                        nc.scalar.activation(qT_h[:, uj % 2, half * 4:half * 4 + 4, :].rearrange("p c n -> p (c n)"), m0[:], ACT.Copy).then_inc(qTh_ready, 1)
                for grp, at in ((0, 2), (1, 10)):
                    if real(b, j, -1) and h == at:
                        ob, oj = where(b, j, -1)
                        O = tile_of(ob, oj)
                        need(act, pv_made, O * PAIRS + 4 * grp + 4)
                        need(act, out_made, O)
                        nc.scalar.activation(oT_h[:, grp * 4:grp * 4 + 4, :].rearrange("p c n -> p (c n)"), o_bank[:], ACT.Copy).then_inc(oTh_ready, 1)
                if real(b, j, -1) and h == P0T_AT + 1:
                    ob, oj = where(b, j, -1)
                    need(act, null_pT_made, tile_of(ob, oj) + 1)
                    need(act, out_made, tile_of(ob, oj))
                    nc.scalar.activation(null_pT[:], m1[0:H, 0:P], ACT.Copy).then_inc(null_pT_ready, 1)
                if up and h == KT_AT + 1:
                    need(act, kT_made, U + 1)
                    if uj == 0:
                        need(act, scores_made, U * H)
                    nc.scalar.activation(kT_h[:, uj * P:(uj + 1) * P], m0[:, 0:P], ACT.Copy).then_inc(kTh_ready, 1)
                if real(b, j):
                    T, n = tile_of(b, j), (j + 1) * P
                    need(act, biased, T * H + h + 1)
                    nc.scalar.activation(probs[:, h, 0:n], probs[:, h, 0:n], ACT.Exp, bias=neg_max[:, j % 2, h:h + 1],
                                         scale=-1.0, accum_out=sums[:, j % 2, h:h + 1]).then_inc(exp_done, 1)
                    if h % QUAD == QUAD - 1:
                        q = slice(h - QUAD + 1, h + 1)
                        need(act, null_d_done, T * QUAD + h // QUAD + 1)
                        nc.scalar.activation(null_e[:, j % 2, q], null_d[:, j % 2, q], ACT.Exp).then_inc(null_e_done, 1)

            run(act, step)

        @block.vector
        def _(dve):
            linked = [0]

            def link(ins):
                linked[0] += 1
                ins.then_inc(mlp_link, 1)
                dve.wait_ge(mlp_link, linked[0])

            dve.wait_ge(dma_small, 9 * 16)
            dve.wait_ge(zeroed, 1)
            for i in range(2):
                rows = slice(i * DH, (i + 1) * DH)
                flat = v_null_sel.rearrange("p a h -> p (a h)")
                link(nc.vector.tensor_copy(flat[rows, i:i + (PAIRS - 1) * (H + 2) + 1:H + 2], v_null[rows, :].to_broadcast([DH, PAIRS])))
            link(nc.vector.tensor_scalar(neg_null_bias[:], neg_null_bias[:], -1.0, None, ALU.mult))
            link(nc.vector.scalar_tensor_tensor(qk_scale[:], qk_tmp[:, 0, :], SCALE, qk_tmp[:, 1, :], ALU.mult, ALU.mult))
            nc.vector.tensor_tensor(k_null_sq, k_null, k_null, ALU.mult).then_inc(v_null_placed, 1)
            dve.wait_ge(v_null_placed, 1)
            link(nc.vector.tensor_reduce(norm2[:, 0, 0:1], k_null_sq, AX.X, ALU.add))
            nc.vector.tensor_scalar(norm2c[:, 0, 0:1], norm2[:, 0, 0:1], L2_EPS ** 2, None, ALU.max).then_inc(k_null_ve, 1)

            def layer_norm(layer):
                for t in range(NT):
                    link(nc.vector.bn_stats(s_st[:, t, :], mlp_h[:, t, :]))
                    link(nc.vector.bn_aggr(s_mv[:, t, :], s_st[:, t, :]))
                nc.vector.tensor_scalar(s_ve[:], s_mv[:, :, 1], LN_EPS, None, ALU.add).then_inc(mlp_ve, 1)
                dve.wait_ge(mlp_rs, layer + 1)
                for t in range(NT):
                    link(nc.vector.tensor_scalar(mlp_h[:, t, :], mlp_h[:, t, :], s_mv[:, t, 0:1], s_rs[:, t:t + 1], ALU.subtract, ALU.mult))
                    nc.vector.tensor_tensor(mlp_h[:, t, :], mlp_h[:, t, :], mlp_g[layer], ALU.mult).then_inc(mlp_affine, 1)
                for t in range(NT):
                    dve.wait_ge(mlp_tanh, NT * layer + t + 1)
                    nc.vector.scalar_tensor_tensor(mlp_h[:, t, :], tanh[(t + layer) % 3], 1.0, mlp_h[:, t, :], ALU.add, ALU.mult).then_inc(mlp_silu, 1)

            dve.wait_ge(dma_mlp, 7 * 16)
            dve.wait_ge(pos_made, 1)
            for t in range(NT):
                link(nc.vector.scalar_tensor_tensor(mlp_h[:, t, :], mlp_w0, pos[:, t:t + 1], mlp_b[0], ALU.mult, ALU.add))
            layer_norm(0)
            dve.wait_ge(k_null_rs, 1)
            link(nc.vector.scalar_tensor_tensor(k_null, k_null, rnorm[:, 0, 0:1], qk_scale[:], ALU.mult, ALU.mult))
            dve.wait_ge(dma_wq, 16)
            for c in range(DC):
                both = squares[:].rearrange("p a n -> p (a n)").rearrange("p (h d) -> p h d", d=DH)
                link(nc.vector.tensor_tensor(both, wq_stage[:, c, :].rearrange("p (h d) -> p h d", d=DH),
                                             k_null.unsqueeze(1).to_broadcast([P, H, DH]), ALU.mult))
                nc.vector.tensor_reduce(wkv_f[:, c, 2 * DH:KVN], both, AX.X, ALU.add).then_inc(wk_null, 1)
                dve.wait_ge(wk_null, c + 1)
                dve.wait_ge(wqh_made, c + 1)
                last = nc.vector.scalar_tensor_tensor(wq_l[:, c, :], wq_stage[:, c, :], g_norm_c[:, c:c + 1], wq_h[:, c, :], ALU.mult, ALU.subtract)
            last.then_inc(dve_staged, 1)
            for t in range(NT):
                dve.wait_ge(h2_made, t + 1)
                link(nc.vector.tensor_tensor(mlp_h[:, t, :], psum[t][:], mlp_b[1], ALU.add))
            layer_norm(1)
            dve.wait_ge(woh_made, 1)
            lo_half(nc.vector, wo_l[:].rearrange("p c n -> p (c n)"), wout_stage.rearrange("p c n -> p (c n)"),
                    wo_h[:].rearrange("p c n -> p (c n)")).then_inc(dve_staged, 1)
            dve.wait_ge(table_made, 1)
            nc.vector.memset(table[:, S:TW], MASKED).then_inc(table_tail, 1)
            nc.vector.tensor_scalar(table[:, 0:S], psum[0][0:H, :], b2_c[:], None, ALU.add).then_inc(table_ready, 1)
            dve.wait_ge(wkh_made, DC)
            for c in range(DC):
                last = nc.vector.scalar_tensor_tensor(wk_l[:, c, :], wkv_f[:, c, :], g_norm_c[:, c:c + 1], wk_h[:, c, :], ALU.mult, ALU.subtract)
            last.then_inc(dve_staged, 1)
            for h in range(1, H, 2):
                dve.wait_ge(flipped, h + 1)
                nc.vector.tensor_copy(bias[:, h, :], psum[h % 8][:]).then_inc(bias_odd, 1)


            def step(b, j, h):
                bb, jj, hh, there = head_at(b, j, h, LAG_T)
                if there and hh % 2:
                    T = tile_of(bb, jj)
                    need(dve, pT_made, T * H + hh + 1)
                    need(dve, pv_made, T * PAIRS + hh // 2 - PR // 2 + 1)
                    n = (jj + 1) * P
                    nc.vector.tensor_copy(probs[:, TR + hh % PR, 0:n], pT_bank[1][:, 0:n]).then_inc(pT_odd, 1)
                up, (ub, uj) = real(b, j, 1), where(b, j, 1)
                U = tile_of(ub, uj)
                if up and h == X_AT + 1:
                    need(dve, xTh_ready, U + 1)
                    lo_half(nc.vector, xT_l[:].rearrange("p c n -> p (c n)"), m0[:], xT_h[:].rearrange("p c n -> p (c n)")).then_inc(xTl_ready, 1)
                for half, at in ((0, Q0_AT), (1, Q1_AT)):
                    if up and h == at + 2:
                        need(dve, q_sq, 2 * U + half + 1)
                        nc.vector.tensor_reduce(norm2[:, uj % 2, half * 8:half * 8 + 8],
                                                squares[:, half, :].rearrange("p (a d) -> p a d", d=DH),
                                                AX.X, ALU.add).then_inc(norm2_done, 1)
                if up and h == Q1_AT + 2:
                    need(dve, norm2_done, 2 * U + 2)
                    need(dve, k_sq, U + 1)
                    nc.vector.tensor_scalar(norm2c[:, uj % 2, :], norm2[:, uj % 2, :], L2_EPS ** 2, None, ALU.max).then_inc(norm2c_done, 1)
                if up and h == QT0_AT - 1:
                    need(dve, rnorm_done, U + 1)
                    need(dve, qT_made, 2 * U)
                    for half, bank in ((0, m0), (1, m1)):
                        r = rnorm[:, uj % 2, half * 8:half * 8 + 8].unsqueeze(2).to_broadcast([P, 8, DH])
                        nc.vector.tensor_tensor(q_norm[:, half * HALF:(half + 1) * HALF].rearrange("p (a d) -> p a d", d=DH),
                                                bank[:].rearrange("p (a d) -> p a d", d=DH), r, ALU.mult).then_inc(q_norm_done, 1)
                    need(dve, kT_made, U)
                    need(dve, kv_copied, U + 1)
                    nc.vector.scalar_tensor_tensor(k_norm[:], kv[:, uj % 2, 0:DH].unsqueeze(1).to_broadcast([P, 2, DH]),
                                                   rnorm[:, uj % 2, H:H + 1], qk_scale[:].unsqueeze(1).to_broadcast([P, 2, DH]),
                                                   ALU.mult, ALU.mult).then_inc(k_norm_done, 1)
                for half, at in ((0, QT0_AT), (1, QT1_AT)):
                    if up and h == at + 1:
                        need(dve, qTh_ready, 2 * U + half + 1)
                        lo_half(nc.vector, qT_l[:, uj % 2, half * 4:half * 4 + 4, :].rearrange("p c n -> p (c n)"), m0[:],
                                qT_h[:, uj % 2, half * 4:half * 4 + 4, :].rearrange("p c n -> p (c n)")).then_inc(qTl_ready, 1)
                for grp, at in ((0, 2), (1, 10)):
                    if real(b, j, -1) and h == at:
                        ob, oj = where(b, j, -1)
                        need(dve, oTh_ready, 2 * tile_of(ob, oj) + grp + 1)
                        lo_half(nc.vector, oT_l[:, grp * 4:grp * 4 + 4, :].rearrange("p c n -> p (c n)"), o_bank[:],
                                oT_h[:, grp * 4:grp * 4 + 4, :].rearrange("p c n -> p (c n)")).then_inc(oTl_ready, 1)
                if real(b, j, 2):
                    lb, lj = where(b, j, 2)
                    L = tile_of(lb, lj)
                    if h == 10:
                        need(dve, x_loaded[lj], 16 * (lb + 1))
                        nc.vector.bn_stats(x_st[:], x_in[:, lj, :]).then_inc(x_st_done, 1)
                        need_apart(dve, x_st_done, L + 1)
                        nc.vector.bn_aggr(x_mv[:], x_st[:]).then_inc(x_mv_done, 1)
                        need(dve, x_mv_done, L + 1)
                        nc.vector.tensor_scalar(x_ve[:], x_mv[:, 1:2], LN_EPS, None, ALU.add).then_inc(x_ve_done, 1)
                    if h == 13:
                        need(dve, x_rs_done, L + 1)
                        need(dve, xT_made, L)
                        nc.vector.tensor_scalar(x_norm[:], x_in[:, lj, :], x_mv[:, 0:1], x_rs[:], ALU.subtract, ALU.mult).then_inc(x_norm_done, 1)
                ob, oj = where(b, j, -1)
                O = tile_of(ob, oj)
                if real(b, j, -1) and h == OUT_AT + 1:
                    need(dve, out_made, O + 1)
                    nc.vector.bn_stats(o_st[:], m1[:]).then_inc(o_st_done, 1)
                    need_apart(dve, o_st_done, O + 1)
                    nc.vector.bn_aggr(o_mv[:], o_st[:]).then_inc(o_mv_done, 1)
                    need(dve, o_mv_done, O + 1)
                    nc.vector.tensor_scalar(o_ve[:], o_mv[:, 1:2], LN_EPS, None, ALU.add).then_inc(o_ve_done, 1)
                if real(b, j, -1) and h == OUT_AT + 2:
                    need(dve, y_stored[oj % 2], 16 * (ob * (NT // 2) + oj // 2))
                    nc.vector.scalar_tensor_tensor(y[:, oj % 2, :], m1[:], o_mv[:, 0:1], g_out_b[:], ALU.subtract, ALU.mult).then_inc(z_done, 1)
                if up and h == KT_AT + 1:
                    if uj == 0:
                        need(dve, mask_loaded, 16 * (ub + 1))
                        need(dve, scores_made, U * H)
                        nc.vector.tensor_scalar(mask_b[:], mask_u8[:], 1.0, -MASKED, ALU.subtract, ALU.mult).then_inc(mask_ready, 1)
                    need(dve, kTh_ready, U + 1)
                    lo_half(nc.vector, kT_l[:, uj * P:(uj + 1) * P], m0[:, 0:P], kT_h[:, uj * P:(uj + 1) * P]).then_inc(kTl_ready, 1)
                if real(b, j):
                    T, n = tile_of(b, j), (j + 1) * P
                    if h == 0:
                        need(dve, neg_null_s_done, T + 1)
                    need(dve, scores_made, T * H + h + 1)
                    need_apart(dve, pT_made, (T - 1) * H + h + 1)
                    nc.vector.tensor_tensor_reduce(out=probs[:, h, 0:n], in0=score_bank[(j * H + h) % SR][:, 0:n],
                                                   in1=bias[:, h, S - n:S], scale=-1.0,
                                                   scalar=neg_null_s[:, j % 2, h:h + 1], op0=ALU.add, op1=ALU.min,
                                                   accum_out=neg_max[:, j % 2, h:h + 1]).then_inc(biased, 1)
                    if h % QUAD == QUAD - 1:
                        q = slice(h - QUAD + 1, h + 1)
                        need(dve, biased, T * H + h + 1)
                        nc.vector.tensor_tensor(null_d[:, j % 2, q], neg_max[:, j % 2, q], neg_null_s[:, j % 2, q], ALU.subtract).then_inc(null_d_done, 1)
                qb, qj, qh, there = head_at(b, j, h, 1)
                if there and h % QUAD == 0:
                    Q = tile_of(qb, qj) * 4 + qh // QUAD
                    q = slice(qh - QUAD + 1, qh + 1)
                    need(dve, null_e_done, Q + 1)
                    nc.vector.tensor_tensor(den[:, qj % 2, q], sums[:, qj % 2, q], null_e[:, qj % 2, q], ALU.add).then_inc(den_done, 1)
                    need(dve, den_done, Q + 1)
                    nc.vector.reciprocal(rden[:, qj % 2, q], den[:, qj % 2, q]).then_inc(rden_done, 1)
                if real(b, j, -1) and h == OUT_AT + 2:
                    need(dve, z_done, O + 1)
                    need(dve, o_rs_done, O + 1)
                    nc.vector.scalar_tensor_tensor(y[:, oj % 2, :], y[:, oj % 2, :], o_rs[:], x_in[:, oj, :], ALU.mult, ALU.add).then_inc(y_done, 1)

            run(dve, step)

        @block.gpsimd
        def _(pool):
            nc.gpsimd.memset(v_null_sel, 0.0).then_inc(zeroed, 1)
            nc.gpsimd.memset(ident[:], 0.0).then_inc(zeroed, 1)
            nc.gpsimd.memset(flip[:], 0.0).then_inc(zeroed, 1)
            nc.gpsimd.memset(neg_half[:], -0.5).then_inc(zeroed, 1)
            nc.gpsimd.memset(ones64[:], 1.0 / DH).then_inc(zeroed, 1)
            nc.gpsimd.iota(pos[:], pattern=[[-P, NT]], base=S - 1, channel_multiplier=-1,
                           allow_small_or_imprecise_dtypes=True).then_inc(pos_made, 1)
            pool.wait_ge(zeroed, 5)
            nc.gpsimd.affine_select(out=ident[:], in_=ident[:], compare_op=ALU.not_equal, fill=1.0, base=0,
                                    pattern=[[-1, P]], channel_multiplier=1).then_inc(ident_made, 1)
            nc.gpsimd.affine_select(out=flip[:], in_=flip[:], compare_op=ALU.not_equal, fill=1.0, base=1 - P,
                                    pattern=[[1, P]], channel_multiplier=1).then_inc(ident_made, 1)
            pool.wait_ge(k_null_ve, 1)
            nc.gpsimd.tensor_tensor(rnorm[:, 0, 0:1], norm2c[:, 0, 0:1], neg_half[:, 0:1], ALU.pow).then_inc(k_null_rs, 1)
            for layer in range(2):
                pool.wait_ge(mlp_ve, layer + 1)
                nc.gpsimd.tensor_tensor(s_rs[:], s_ve[:], neg_half[:, 0:NT], ALU.pow).then_inc(mlp_rs, 1)


            def step(b, j, h):
                qb, qj, qh, there = head_at(b, j, h, 1)
                if there and h % QUAD == 0:
                    T, n = tile_of(qb, qj), (qj + 1) * P
                    need(pool, rden_done, T * 4 + qh // QUAD + 1)
                    for i in range(2):
                        lo = qh - 3 + 2 * i
                        nc.gpsimd.tensor_tensor(probs[:, lo:lo + 2, 0:n], probs[:, lo:lo + 2, 0:n],
                                                rden[:, qj % 2, lo:lo + 2].unsqueeze(2).to_broadcast([P, 2, n]), ALU.mult).then_inc(scaled, 1)
                        if i == 0:
                            q = slice(qh - 3, qh + 1)
                            need(pool, null_pT_made, T - 1)
                            nc.gpsimd.tensor_tensor(null_p[:, qj % 2, q], null_e[:, qj % 2, q], rden[:, qj % 2, q], ALU.mult).then_inc(null_p_done, 1)
                up, (ub, uj) = real(b, j, 1), where(b, j, 1)
                U = tile_of(ub, uj)
                if up and h == Q1_AT + 2:
                    need(pool, norm2c_done, U + 1)
                    nc.gpsimd.tensor_tensor(rnorm[:, uj % 2, :], norm2c[:, uj % 2, :], neg_half[:], ALU.pow).then_inc(rnorm_done, 1)
                    need(pool, kv_copied, U + 1)
                    need(pool, rnorm_done, U + 1)
                    nc.gpsimd.tensor_tensor(null_s[:], kv[:, uj % 2, 2 * DH:KVN], rnorm[:, uj % 2, 0:H], ALU.mult).then_inc(null_s_done, 1)
                    need(pool, null_s_done, U + 1)
                    nc.gpsimd.tensor_tensor(neg_null_s[:, uj % 2, :], neg_null_bias[:], null_s[:], ALU.subtract).then_inc(neg_null_s_done, 1)
                if real(b, j) and h == 10:
                    T = tile_of(b, j)
                    if j == 0:
                        need(pool, pv_made, T * PAIRS)
                    need_apart(pool, kv_copied, T + 1)
                    nc.gpsimd.tensor_copy(v[:, j, :], kv[:, j % 2, DH:2 * DH]).then_inc(v_copied, 1)
                if real(b, j, 2) and h == 11:
                    lb, lj = where(b, j, 2)
                    need(pool, x_ve_done, tile_of(lb, lj) + 1)
                    nc.gpsimd.tensor_tensor(x_rs[:], x_ve[:], neg_half[:, 0:1], ALU.pow).then_inc(x_rs_done, 1)
                if real(b, j, -1) and h == OUT_AT + 1:
                    ob, oj = where(b, j, -1)
                    need(pool, o_ve_done, tile_of(ob, oj) + 1)
                    nc.gpsimd.tensor_tensor(o_rs[:], o_ve[:], neg_half[:, 0:1], ALU.pow).then_inc(o_rs_done, 1)

            run(pool, step)


_INS = ['x', 'cond_64', 'mask_BxS_bf1', 'L0_cond_g_norm', 'L0_cond_Wq', 'L0_cond_Wkv', 'L0_cond_q_scale',
        'L0_cond_k_scale', 'L0_cond_null_attn_bias', 'L0_cond_w0', 'L0_cond_b0', 'L0_cond_g0', 'L0_cond_w1',
        'L0_cond_b1', 'L0_cond_g1', 'L0_cond_w2', 'L0_cond_b2', 'L0_cond_Wout', 'L0_cond_g_out']


def kernel(**inputs):
    import numpy as np
    import concourse.bacc as bacc
    from concourse.bass_utils import run_bass_kernel_spmd

    nc = bacc.Bacc("TRN2", target_bir_lowering=False, num_devices=1)
    arrays, args = {}, []
    for name in _INS:
        a = np.ascontiguousarray(inputs[name])
        if a.dtype == np.bool_:
            a = a.view(np.uint8)
        arrays[f"in_{name}"] = a
        args.append(nc.dram_tensor(f"in_{name}", a.shape, mybir.dt.from_np(a.dtype), kind="ExternalInput").ap())
    S, H = inputs['x'].shape[1], inputs['L0_cond_null_attn_bias'].shape[0]
    args.append(nc.dram_tensor("bias_table", (H, S + 128), mybir.dt.float32, kind="Internal").ap())
    args.append(nc.dram_tensor("out", inputs['x'].shape, mybir.dt.float32, kind="ExternalOutput").ap())
    cond_attention_kernel(nc, *args)
    r = run_bass_kernel_spmd(nc, [arrays], core_ids=[0])
    return r.results[0]["out"]
```

```python
import concourse.bass as bass
from concourse import mybir
from contextlib import ExitStack


def cond_attention_kernel(nc, x, cond, mask, g_norm, wq, wkv, q_scale, k_scale, null_bias,
                          w0, b0, g0, w1, b1, g1, w2, b2, wout, g_out, table_dram, out):
    f32, f32r, u8 = mybir.dt.float32, mybir.dt.float32r, mybir.dt.uint8
    ALU = mybir.AluOpType
    ACT = mybir.ActivationFunctionType
    AX = mybir.AxisListType

    P = 128
    B, S, D = x.shape
    NT = S // P
    TILES = B * NT
    DC = D // P
    DH = q_scale.shape[0]
    H = null_bias.shape[0]
    INNER = H * DH
    PAIRS = H // 2
    HALF = INNER // 2
    KVN = 2 * DH + H
    QUAD = 4
    TW = S + P
    SCALE, LN_EPS, L2_EPS = 8.0, 1e-5, 1e-12
    MASKED = -1.5e38
    LAG_T, LAG_V = 8, 9
    TR, PR, SR = 16, 4, 3

    X_AT, KV_AT, NULL_AT, KT_AT = 1, 3, 3, 11
    Q_AT = ((5, 5, 6, 6), (8, 8, 8, 9))
    Q_DONE = (6, 9)
    OUT_AT, OUT_DONE = (9, 10, 10, 11, 12, 12, 13, 14), 14
    FINISH_AT, Z_AT, Y_AT = 15, 15, 19
    NORM_AT, NORM_TILE = (10, 11, 14, 2), (1, 1, 1, 0)
    QT_AT, QT_TILE = (13, 15, 2, 4), (1, 1, 0, 0)
    STATS_AT, X_NORM_AT = 6, 8

    x_v = x.rearrange("b (t p) d -> b t p d", p=P)
    out_v = out.rearrange("b (t p) d -> b t p d", p=P)

    ctx = ExitStack()
    with ctx:
        def sb(name, shape, dt=f32):
            return ctx.enter_context(nc.sbuf_tensor(name, shape, dt))

        def sem(name):
            return ctx.enter_context(nc.semaphore(name))

        wq_h, wq_l = sb("wq_h", [P, DC, INNER], f32r), sb("wq_l", [P, DC, INNER], f32r)
        wk_h, wk_l = sb("wk_h", [P, DC, KVN], f32r), sb("wk_l", [P, DC, KVN], f32r)
        wo_h, wo_l = sb("wo_h", [P, PAIRS, D], f32r), sb("wo_l", [P, PAIRS, D], f32r)
        bias = sb("bias", [P, H, S])
        null_w = sb("null_w", [96, D], f32r)
        ident, flip = sb("ident", [P, P]), sb("flip", [P, P])
        g_out_b = sb("g_out_b", [P, D])
        qk_scale = sb("qk_scale", [P, DH])
        neg_null_bias = sb("neg_null_bias", [P, H])
        neg_half = sb("neg_half", [P, H + 1])
        x_in = sb("x_in", [P, 4, D])
        x_norm = sb("x_norm", [P, D])
        xT_h, xT_l = sb("xT_h", [P, DC, P], f32r), sb("xT_l", [P, DC, P], f32r)
        kv = sb("kv", [P, 2, KVN])
        q_raw = sb("q_raw", [P, INNER])
        k_squares = sb("k_squares", [P, DH])
        norm2 = sb("norm2", [P, 2, H + 1])
        norm2c = sb("norm2c", [P, 2, H + 1])
        rnorm = sb("rnorm", [P, 2, H + 1])
        q_norm = sb("q_norm", [P, H // 2, 2, DH])
        k_norm = sb("k_norm", [P, 2, DH])
        null_s = sb("null_s", [P, H])
        neg_null_s = sb("neg_null_s", [P, 2, H])
        q_hh, q_l1 = sb("q_hh", [P, H, P], f32r), sb("q_l1", [P, H, P], f32r)
        k_hl, k_hm = sb("k_hl", [P, S], f32r), sb("k_hm", [P, S], f32r)
        k_first = sb("k_first", [P, 2, P], f32r)
        v = sb("v", [P, NT, DH])
        mask_u8 = sb("mask_u8", [P, S], u8)
        probs = sb("probs", [P, TR + PR, S])
        neg_max, sums, null_e = sb("neg_max", [P, 2, H]), sb("sums", [P, 2, H]), sb("null_e", [P, 2, H])
        null_d, den, rden = sb("null_d", [P, 2, H]), sb("den", [P, 2, H]), sb("rden", [P, 2, H])
        null_p = sb("null_p", [P, 2, 3, 32])
        null_pT = sb("null_pT", [96, P], f32r)
        oT_h, oT_l = sb("oT_h", [P, PAIRS, P], f32r), sb("oT_l", [P, PAIRS, P], f32r)
        y = sb("y", [P, 2, D])
        x_st, x_mv, x_ve, x_rs = sb("x_st", [P, 6]), sb("x_mv", [P, 2]), sb("x_ve", [P, 1]), sb("x_rs", [P, 1])
        o_st, o_mv, o_ve, o_rs = sb("o_st", [P, 6]), sb("o_mv", [P, 2]), sb("o_ve", [P, 1]), sb("o_rs", [P, 1])
        g_norm_c, b2_c, v_null = sb("g_norm_c", [P, DC]), sb("b2_c", [H, 1]), sb("v_null", [P, 1])
        w2_sb, pos = sb("w2_sb", [P, DC, H]), sb("pos", [P, NT])
        s_st, s_mv, s_ve, s_rs = sb("s_st", [P, NT, 6]), sb("s_mv", [P, NT, 2]), sb("s_ve", [P, NT]), sb("s_rs", [P, NT])

        psum = [ctx.enter_context(nc.psum_tensor(f"bank{i}", [P, 512], f32)) for i in range(8)]
        score_bank, pT_bank, o_bank, m0, m1 = psum[0:SR], psum[SR:SR + 2], psum[5], psum[6], psum[7]

        x_loaded = [sem(f"x_loaded{i}") for i in range(4)]
        y_stored = [sem(f"y_stored{i}") for i in range(2)]
        mask_loaded = sem("mask_loaded")
        xT_made, kv_made, qT_made = sem("xT_made"), sem("kv_made"), sem("qT_made")
        kT_made, null_pT_made, out_made = sem("kT_made"), sem("null_pT_made"), sem("out_made")
        scores_made, pT_made, pv_made = sem("scores_made"), sem("pT_made"), sem("pv_made")
        xTh_ready, kv_copied, k_sq = sem("xTh_ready"), sem("kv_copied"), sem("k_sq")
        q_copied = [sem(f"q_copied{i}") for i in range(2)]
        k_hl_lo, k_norm2c_done, k_rnorm_done = sem("k_hl_lo"), sem("k_norm2c_done"), sem("k_rnorm_done")
        q_norm_twice, oT_used = sem("q_norm_twice"), sem("oT_used")
        q_made, q_sq, norm2_done = ([sem(f"{n}{i}") for i in range(2)] for n in ("q_made", "q_sq", "norm2_done"))
        qTh_ready, kTh_ready, null_pT_ready = sem("qTh_ready"), sem("kTh_ready"), sem("null_pT_ready")
        exp_done, null_e_done, pT_even, oTh_ready = sem("exp_done"), sem("null_e_done"), sem("pT_even"), sem("oTh_ready")
        x_st_done, x_mv_done, x_ve_done, x_norm_done = sem("x_st_done"), sem("x_mv_done"), sem("x_ve_done"), sem("x_norm_done")
        xTl_ready, norm2c_done, q_norm_done = sem("xTl_ready"), sem("norm2c_done"), sem("q_norm_done")
        k_norm_done, qTl_ready, kTl_ready, k_first_copied = sem("k_norm_done"), sem("qTl_ready"), sem("kTl_ready"), sem("k_first_copied")
        biased, null_d_done, den_done, rden_done = sem("biased"), sem("null_d_done"), sem("den_done"), sem("rden_done")
        pT_odd, oTl_ready = sem("pT_odd"), sem("oTl_ready")
        o_st_done, o_mv_done, o_ve_done, z_done, y_done = sem("o_st_done"), sem("o_mv_done"), sem("o_ve_done"), sem("z_done"), sem("y_done")
        x_rs_done, rnorm_done, null_s_done, neg_null_s_done = sem("x_rs_done"), sem("rnorm_done"), sem("null_s_done"), sem("neg_null_s_done")
        scaled, null_p_done, v_copied, o_rs_done = sem("scaled"), sem("null_p_done"), sem("v_copied"), sem("o_rs_done")
        passed = sem("passed")
        null_pT_hi = sem("null_pT_hi")
        dma_wq, dma_wout, dma_wkv, dma_small, dma_mlp = sem("dma_wq"), sem("dma_wout"), sem("dma_wkv"), sem("dma_small"), sem("dma_mlp")
        table_stored, table_back = sem("table_stored"), [sem(f"table_back{i}") for i in range(4)]
        zeroed, table_tail, ident_made, pos_made = sem("zeroed"), sem("table_tail"), sem("ident_made"), sem("pos_made")
        k_null_ve, k_null_rs, v_null_placed = sem("k_null_ve"), sem("k_null_rs"), sem("v_null_placed")
        mlp_link, mlp_ve, mlp_rs, mlp_affine = sem("mlp_link"), sem("mlp_ve"), sem("mlp_rs"), sem("mlp_affine")
        mlp_tanh, mlp_silu, hT_made, hT_ready, h2_made = sem("mlp_tanh"), sem("mlp_silu"), sem("hT_made"), sem("hT_ready"), sem("h2_made")
        wqh_made, wkh_made, woh_made, wk_null = sem("wqh_made"), sem("wkh_made"), sem("woh_made"), sem("wk_null")
        dve_staged = sem("dve_staged")
        null_w_made, null_w_ready = sem("null_w_made"), sem("null_w_ready")
        null_w_hi, null_w_lo = sem("null_w_hi"), sem("null_w_lo")
        table_made, table_ready = sem("table_made"), sem("table_ready")
        flipped, bias_even, bias_odd = sem("flipped"), sem("bias_even"), sem("bias_odd")

        q_norm_flat = q_norm[:].rearrange("p a b d -> p (a b d)")
        v_null_sel = q_norm_flat[:, 0:PAIRS * H].rearrange("p (a h) -> p a h", a=PAIRS)
        k_null, k_null_sq = q_norm_flat[:, 512:512 + DH], q_norm_flat[:, 576:576 + DH]
        qk_tmp = q_norm_flat[:, 640:640 + 2 * DH].rearrange("p (a d) -> p a d", a=2)
        table = q_raw[0:H, 0:TW]
        null_w_tmp = x_norm[0:H, :]
        wkv_f = y[:].rearrange("p a n -> p (a n)")[:, 0:DC * KVN].rearrange("p (c n) -> p c n", c=DC)
        wq_stage = probs[:, 0:8, :].rearrange("p (c a) n -> p c (a n)", c=DC)
        wout_stage = probs[:, 8:16, :]
        hT = probs[:, 16:20, :]
        mlp_h, mlp_w1, mlp_w0 = bias[:, 0:4, :], bias[:, 4:8, :], bias[:, 8, :]
        mlp_b, mlp_g = (bias[:, 9, :], bias[:, 11, :]), (bias[:, 10, :], bias[:, 12, :])
        tanh = [bias[:, 13 + i, :] for i in range(3)]

        block = ctx.enter_context(nc.Block())

        def need(eng, semaphore, value):
            if not isinstance(value, int) or value > 0:
                eng.wait_ge(semaphore, value)

        def need_apart(eng, semaphore, value):
            need(eng, semaphore, value)
            if not isinstance(value, int):
                eng.sem_inc(passed, 1)

        def tile_of(b, j):
            return b * NT + j

        def real(b, j, offset=0):
            return not isinstance(b, int) or 0 <= b * NT + j + offset < TILES

        def where(b, j, offset):
            return b + (j + offset) // NT, (j + offset) % NT

        def run(eng, step):
            for t in range(-2, NT):
                for h in range(H):
                    step(t // NT, t % NT, h)
            with eng.Fori(1, B - 1) as b:
                for j in range(NT):
                    for h in range(H):
                        step(b, j, h)
            for t in range((B - 1) * NT, B * NT + 1):
                for h in range(H):
                    step(t // NT, t % NT, h)

        def ring_before(s, ring):
            return s - ring if s >= ring else max(o for o in range(NT * H) if o % ring == s % ring) - NT * H

        def head_at(b, j, h, lag):
            off, hh = (h - lag) // H, (h - lag) % H
            bb, jj = where(b, j, off)
            return bb, jj, hh, real(b, j, off)

        def new_keys(uj):
            if uj == 0:
                return k_first[:, 0, :], k_first[:, 1, :]
            return k_hl[:, uj * P:(uj + 1) * P], k_hm[:, uj * P:(uj + 1) * P]

        def lo_half(eng, dst, src, hi):
            return eng.tensor_tensor(dst, src, hi.bitcast(f32), ALU.subtract)

        @block.sync
        def _(sp):
            def bcast(ap, n=P):
                return ap.partition_broadcast(n)

            sp.dma_start(g_norm_c[:], g_norm.rearrange("(c p) -> p c", p=P), allow_slow_non_contiguous=True).then_inc(dma_small, 16)
            sp.dma_start(k_null, bcast(cond[0, :])).then_inc(dma_small, 16)
            sp.dma_start(qk_tmp[:, 0, :], bcast(q_scale)).then_inc(dma_small, 16)
            sp.dma_start(qk_tmp[:, 1, :], bcast(k_scale)).then_inc(dma_small, 16)
            for i in range(2):
                sp.dma_start(v_null[i * DH:(i + 1) * DH, :], cond[1, :].rearrange("(p a) -> p a", a=1)).then_inc(dma_small, 16)
            sp.dma_start(neg_null_bias[:], bcast(null_bias)).then_inc(dma_small, 16)
            sp.dma_start(b2_c[:], b2.rearrange("(p a) -> p a", a=1)).then_inc(dma_small, 16)
            sp.dma_start(g_out_b[:], bcast(g_out)).then_inc(dma_small, 16)
            for place, w in ((mlp_w0, w0[0, :]), (mlp_b[0], b0), (mlp_g[0], g0), (mlp_b[1], b1), (mlp_g[1], g1)):
                sp.dma_start(place, bcast(w)).then_inc(dma_mlp, 16)
            sp.dma_start(mlp_w1, w1.rearrange("(c p) n -> p c n", p=P)).then_inc(dma_mlp, 16)
            sp.dma_start(w2_sb[:], w2.rearrange("(c p) n -> p c n", p=P)).then_inc(dma_mlp, 16)
            sp.dma_start(wq_stage, wq.rearrange("(c p) n -> p c n", p=P)).then_inc(dma_wq, 16)
            sp.dma_start(wkv_f[:, :, 0:2 * DH], wkv.rearrange("(c p) n -> p c n", p=P)).then_inc(dma_wkv, 16)
            sp.dma_start(wout_stage, wout.rearrange("(c p) n -> p c n", p=P)).then_inc(dma_wout, 16)
            sp.dma_start(x_in[:, 0, :], x_v[0, 0]).then_inc(x_loaded[0], 16)
            sp.wait_ge(table_ready, 1)
            sp.wait_ge(table_tail, 1)
            sp.dma_start(table_dram, table).then_inc(table_stored, 16)
            sp.wait_ge(table_stored, 16)
            sp.wait_ge(dve_staged, 3)
            sp.wait_ge(wqh_made, DC)
            sp.wait_ge(woh_made, 1)
            sp.wait_ge(null_w_made, 1)
            for i in range(4):
                hs = H // 4
                src = bass.AP(table_dram.tensor, i * hs * TW, [[1, P], [TW, hs], [1, S]])
                sp.dma_start(probs[:, i * hs:(i + 1) * hs, :], src).then_inc(table_back[i], 16)

            def step(b, j, h):
                if h == 0 and real(b, j, 3):
                    bb, jj = where(b, j, 3)
                    need_apart(sp, y_done, tile_of(bb, jj) - 4 + 1)
                    sp.dma_start(x_in[:, jj, :], x_v[bb, jj]).then_inc(x_loaded[jj], 16)
                if h == 14 and j == 2 and real(b, j, 2):
                    need_apart(sp, kTl_ready, tile_of(b, j) + 2)
                    sp.dma_start(mask_u8[:], bcast(mask[b + 1, :])).then_inc(mask_loaded, 16)
                if h == H - 1 and real(b, j, -1):
                    bb, jj = where(b, j, -1)
                    need_apart(sp, y_done, tile_of(bb, jj) + 1)
                    sp.dma_start(out_v[bb, jj], y[:, jj % 2, :]).then_inc(y_stored[jj % 2], 16)

            run(sp, step)
            for i in range(2):
                sp.wait_ge(y_stored[i], 16 * TILES // 2)

        @block.tensor
        def _(pe):
            pe.wait_ge(v_null_placed, 1)
            pe.wait_ge(dma_wout, 16)
            for p in range(PAIRS):
                last = nc.tensor.matmul(psum[7][0:H, :], v_null_sel[:, p, :], wout_stage[:, p, :], start=(p == 0), stop=(p == PAIRS - 1))
            last.then_inc(null_w_made, 1)
            pe.wait_ge(ident_made, 2)
            pe.wait_ge(dma_mlp, 7 * 16)
            for layer in range(2):
                pe.wait_ge(mlp_silu, NT * (layer + 1))
                if layer == 1:
                    pe.wait_ge(null_w_ready, 1)
                for c in range(DC):
                    for t in range(NT):
                        last = nc.tensor.transpose(psum[4 * layer + c][:, t * P:(t + 1) * P], mlp_h[:, t, c * P:(c + 1) * P], ident[:])
                    last.then_inc(hT_made, 1)
                pe.wait_ge(hT_ready, DC * (layer + 1))
                if layer == 0:
                    for t in range(NT):
                        for c in range(DC):
                            last = nc.tensor.matmul(psum[t][:], hT[:, c, t * P:(t + 1) * P], mlp_w1[:, c, :], start=(c == 0), stop=(c == DC - 1))
                        last.then_inc(h2_made, 1)
            for c in range(DC):
                last = nc.tensor.matmul(psum[0][0:H, :], w2_sb[:, c, :], hT[:, c, :], start=(c == 0), stop=(c == DC - 1))
            last.then_inc(table_made, 1)
            pe.wait_ge(table_ready, 1)
            for h in range(H):
                if h % 4 == 0:
                    pe.wait_ge(table_back[h // 4], 16)
                if h >= 8:
                    pe.wait_ge(bias_odd if h % 2 else bias_even, (h - 8) // 2 + 1)
                nc.tensor.matmul(psum[h % 8][:], flip[:], probs[:, h, :], start=True, stop=True).then_inc(flipped, 1)
            pe.wait_ge(bias_even, H // 2)
            pe.wait_ge(bias_odd, H // 2)
            pe.wait_ge(dve_staged, 3)
            pe.wait_ge(null_w_ready, 1)
            pe.wait_ge(zeroed, 6)


            def three(dst, a_h, a_l, b_h, b_l, first, last):
                nc.tensor.matmul(dst, a_h, b_h, start=first, stop=False)
                nc.tensor.matmul(dst, a_h, b_l, start=False, stop=False)
                return nc.tensor.matmul(dst, a_l, b_h, start=False, stop=last)

            def piece(b, j, h):
                up, (ub, uj) = real(b, j, 1), where(b, j, 1)
                U = tile_of(ub, uj)
                down, (ob, oj) = real(b, j, -1), where(b, j, -1)
                O = tile_of(ob, oj)
                if h == X_AT and up:
                    need(pe, x_norm_done, U + 1)
                    need(pe, z_done, U - 2)
                    for c in range(DC):
                        last = nc.tensor.transpose(m1[:, c * P:(c + 1) * P], x_norm[:, c * P:(c + 1) * P], ident[:])
                    last.then_inc(xT_made, 1)
                if h == NULL_AT and down:
                    need(pe, null_p_done, 4 * O + 4)
                    if up:
                        need(pe, xTl_ready, U + 1)
                    else:
                        need(pe, z_done, O)
                    nc.tensor.transpose(m1[0:96, 2 * P:3 * P], null_p[:, oj % 2].rearrange("p a h -> p (a h)"), ident[:]).then_inc(null_pT_made, 1)
                if h == KV_AT and up:
                    need(pe, xTl_ready, U + 1)
                    for c in range(DC):
                        last = three(m1[:, 0:KVN], xT_h[:, c, :], xT_l[:, c, :], wk_h[:, c, :], wk_l[:, c, :], c == 0, c == DC - 1)
                    last.then_inc(kv_made, 1)
                for half, bank in ((0, m1), (1, m0)):
                    for c in range(DC):
                        if h == Q_AT[half][c] and up:
                            if c == 0 and half:
                                need(pe, qTl_ready, 4 * U)
                            elif c == 0:
                                need(pe, kv_copied, U + 1)
                                need(pe, null_pT_ready, U - 1)
                            cols = slice(half * HALF, (half + 1) * HALF)
                            last = three(bank[:], xT_h[:, c, :], xT_l[:, c, :], wq_h[:, c, cols], wq_l[:, c, cols], c == 0, c == DC - 1)
                            if c == DC - 1:
                                last.then_inc(q_made[half], 1)
                if h == KT_AT and up:
                    need(pe, k_norm_done, U + 1)
                    need(pe, norm2_done[1], U + 1)
                    nc.tensor.transpose(m0[:, 0:P], k_norm[:].rearrange("p a d -> p (a d)"), ident[:]).then_inc(kT_made, 1)
                for i in range(4):
                    if h == QT_AT[i] and real(b, j, QT_TILE[i]):
                        V = tile_of(*where(b, j, QT_TILE[i]))
                        need(pe, q_norm_done, 4 * V + i + 1)
                        need(pe, q_norm_twice, 4 * V + i + 1)
                        if i == 0:
                            need(pe, k_hl_lo, V + 1)
                        else:
                            need(pe, qTl_ready, 4 * V + i)
                        for k in range(4):
                            last = nc.tensor.transpose(m0[:, k * P:(k + 1) * P], q_norm[:, (i * 4 + k) % 8].rearrange("p a d -> p (a d)"), ident[:])
                        last.then_inc(qT_made, 1)
                for p in range(PAIRS):
                    if h == OUT_AT[p] and down:
                        if p == 0 and up:
                            need(pe, norm2_done[0], U + 1)
                        elif p == 0:
                            need(pe, null_pT_ready, O + 1)
                        if p % 2 == 0:
                            need(pe, oTl_ready, 4 * O + p // 2 + 1)
                        last = three(m1[:], oT_h[:, p, :], oT_l[:, p, :], wo_h[:, p, :], wo_l[:, p, :], p == 0, False)
                        if p % 2:
                            last.then_inc(oT_used, 1)
                        if p == PAIRS - 1:
                            need(pe, null_pT_ready, O + 1)
                            nc.tensor.matmul(m1[:], null_pT[:], null_w[:], start=False, stop=True).then_inc(out_made, 1)

            def step(b, j, h):
                bb, jj, hh, there = head_at(b, j, h, LAG_T)
                if there:
                    s = tile_of(bb, jj) * H + hh
                    need(pe, scaled, tile_of(bb, jj) * PAIRS + hh // 2 + 1)
                    need(pe, pT_odd if hh % 2 else pT_even, tile_of(bb, jj) * PAIRS + hh // 2)
                    for k in range(jj + 1):
                        last = nc.tensor.transpose(pT_bank[hh % 2][:, k * P:(k + 1) * P], probs[:, hh, k * P:(k + 1) * P], ident[:])
                    last.then_inc(pT_made, 1)
                piece(b, j, h)
                bb, jj, hh, there = head_at(b, j, h, LAG_V)
                if there and hh % QUAD == QUAD - 1:
                    T, g = tile_of(bb, jj), hh // QUAD
                    need(pe, pT_even, T * PAIRS + 2 * g + 2)
                    need(pe, pT_odd, T * PAIRS + 2 * g + 2)
                    if g == 0:
                        need(pe, v_copied, T + 1)
                    need(pe, oTl_ready, 4 * T + g)
                    for k in range(jj + 1):
                        for i in range(2):
                            last = nc.tensor.matmul(o_bank[i * DH:(i + 1) * DH, 0:2 * P], v[:, k, :],
                                                    probs[:, TR + i:TR + PR:2, k * P:(k + 1) * P],
                                                    start=(k == 0), stop=(k == jj))
                    last.then_inc(pv_made, 1)
                if real(b, j):
                    T, n = tile_of(b, j), (j + 1) * P
                    if h == 0:
                        need(pe, kTl_ready, T + 1)
                        need(pe, kTh_ready, T + 1)
                        if j == 1:
                            need(pe, k_first_copied, b + 1)
                    if h % QUAD == 0:
                        need(pe, qTl_ready, 4 * T + h // QUAD + 1)
                    before = ring_before(j * H + h, SR)
                    need(pe, biased, b * NT * H + before + 1)
                    bank = score_bank[(j * H + h) % SR]
                    hl, hm = (k_hl[:, 0:n], k_hm[:, 0:n]) if j else new_keys(0)
                    nc.tensor.matmul(bank[:, 0:n], q_hh[:, h, :], hl, start=True, stop=False)
                    nc.tensor.matmul(bank[:, 0:n], q_l1[:, h, :], hm, start=False, stop=True).then_inc(scores_made, 1)

            run(pe, step)

        @block.scalar
        def _(act):
            for t in range(NT):
                act.wait_ge(mlp_affine, t + 1)
                if t == 3:
                    act.wait_ge(mlp_silu, 1)
                nc.scalar.activation(tanh[t % 3], mlp_h[:, t, :], ACT.Tanh, scale=0.5).then_inc(mlp_tanh, 1)
            act.wait_ge(dma_wq, 16)
            act.wait_ge(dma_small, 9 * 16)
            for c in range(DC):
                nc.scalar.activation(wq_h[:, c, :], wq_stage[:, c, :], ACT.Copy, scale=g_norm_c[:, c:c + 1]).then_inc(wqh_made, 1)
            for layer in range(2):
                for c in range(DC):
                    act.wait_ge(hT_made, DC * layer + c + 1)
                    if layer == 1 and c == 0:
                        act.wait_ge(h2_made, NT)
                    nc.scalar.activation(hT[:, c, :], psum[4 * layer + c][:], ACT.Copy, scale=0.5).then_inc(hT_ready, 1)
                if layer == 0:
                    act.wait_ge(dma_wout, 16)
                    nc.scalar.activation(wo_h[:].rearrange("p c n -> p (c n)"), wout_stage.rearrange("p c n -> p (c n)"), ACT.Copy).then_inc(woh_made, 1)
                    act.wait_ge(null_w_made, 1)
                    act.wait_ge(zeroed, 6)
                    for i in range(2):
                        nc.scalar.activation(null_w[32 * i:32 * i + H, :], psum[7][0:H, :], ACT.Copy).then_inc(null_w_hi, 1)
                    act.wait_ge(wk_null, DC)
                    act.wait_ge(dma_wkv, 16)
                    act.wait_ge(null_w_lo, 1)
                    nc.scalar.activation(null_w[64:64 + H, :], null_w_tmp, ACT.Copy).then_inc(null_w_ready, 1)
                    for c in range(DC):
                        nc.scalar.activation(wk_h[:, c, :], wkv_f[:, c, :], ACT.Copy, scale=g_norm_c[:, c:c + 1]).then_inc(wkh_made, 1)
                    for t in range(NT):
                        act.wait_ge(mlp_affine, NT + t + 1)
                        act.wait_ge(mlp_silu, t + (2 if t < 3 else NT + 1 - 3))
                        nc.scalar.activation(tanh[(t + 1) % 3], mlp_h[:, t, :], ACT.Tanh, scale=0.5).then_inc(mlp_tanh, 1)
            for h in range(0, H, 2):
                act.wait_ge(flipped, h + 1)
                nc.scalar.activation(bias[:, h, :], psum[h % 8][:], ACT.Copy).then_inc(bias_even, 1)


            def step(b, j, h):
                bb, jj, hh, there = head_at(b, j, h, LAG_T)
                if there and hh % 2 == 0:
                    T = tile_of(bb, jj)
                    need(act, pT_made, T * H + hh + 1)
                    need(act, pv_made, T * 4 + hh // QUAD)
                    n = (jj + 1) * P
                    nc.scalar.activation(probs[:, TR + hh % PR, 0:n], pT_bank[0][:, 0:n], ACT.Copy).then_inc(pT_even, 1)
                up, (ub, uj) = real(b, j, 1), where(b, j, 1)
                U = tile_of(ub, uj)
                if up and h == X_AT:
                    need(act, xT_made, U + 1)
                    nc.scalar.activation(xT_h[:].rearrange("p c n -> p (c n)"), m1[:], ACT.Copy).then_inc(xTh_ready, 1)
                if real(b, j, -1) and h == NULL_AT:
                    ob, oj = where(b, j, -1)
                    need(act, null_pT_made, tile_of(ob, oj) + 1)
                    if up:
                        need(act, kv_made, U + 1)
                    need(act, out_made, tile_of(ob, oj))
                    nc.scalar.activation(null_pT[:], m1[0:96, 2 * P:3 * P], ACT.Copy).then_inc(null_pT_hi, 1)
                if up and h == KV_AT:
                    need(act, kv_made, U + 1)
                    need(act, v_copied, U - 1)
                    nc.scalar.activation(kv[:, uj % 2, :], m1[:, 0:KVN], ACT.Copy).then_inc(kv_copied, 1)
                    need(act, kv_copied, U + 1)
                    nc.scalar.activation(k_squares[:], kv[:, uj % 2, 0:DH], ACT.Square,
                                         accum_out=norm2[:, uj % 2, H:H + 1]).then_inc(k_sq, 1)
                for half, bank in ((0, m1), (1, m0)):
                    if up and h == Q_DONE[half]:
                        need(act, q_made[half], U + 1)
                        need(act, q_norm_done, 4 * U - 2 + 2 * half)
                        need(act, q_norm_twice, 4 * U - 2 + 2 * half)
                        nc.scalar.activation(q_raw[:, half * HALF:(half + 1) * HALF], bank[:], ACT.Copy).then_inc(q_copied[half], 1)
                        need(act, q_copied[half], U + 1)
                        nc.scalar.activation(bank[:], bank[:], ACT.Square).then_inc(q_sq[half], 1)
                for i in range(4):
                    if h == QT_AT[i] and real(b, j, QT_TILE[i]):
                        V = tile_of(*where(b, j, QT_TILE[i]))
                        need(act, qT_made, 4 * V + i + 1)
                        need(act, scores_made, (V - 1) * H + 4 * i + 4)
                        nc.scalar.activation(q_hh[:, 4 * i:4 * i + 4, :].rearrange("p c n -> p (c n)"), m0[:], ACT.Copy).then_inc(qTh_ready, 1)
                ob, oj, hh, there = head_at(b, j, h, LAG_V)
                if there and hh % QUAD == QUAD - 1:
                    O, g = tile_of(ob, oj), hh // QUAD
                    need(act, pv_made, 4 * O + g + 1)
                    need(act, oT_used, 4 * (O - 1) + g + 1)
                    nc.scalar.activation(oT_h[:, 2 * g:2 * g + 2, :].rearrange("p c n -> p (c n)"), o_bank[:, 0:2 * P], ACT.Copy).then_inc(oTh_ready, 1)
                if up and h == KT_AT:
                    hl, hm = new_keys(uj)
                    need(act, kT_made, U + 1)
                    if uj == 0:
                        need(act, scores_made, (U - 3) * H)
                        need(act, k_first_copied, ub)
                    else:
                        need(act, scores_made, (U - uj) * H)
                    nc.scalar.activation(hl[0:DH, :], m0[0:DH, 0:P], ACT.Copy)
                    nc.scalar.activation(hm, m0[:, 0:P], ACT.Copy).then_inc(kTh_ready, 1)
                if real(b, j) and j == 0 and h == 3:
                    need(act, scores_made, tile_of(b, j) * H)
                    need(act, kTl_ready, tile_of(b, j) + 1)
                    nc.scalar.activation(k_hl[:, 0:P], k_first[:, 0, :].bitcast(f32), ACT.Copy)
                    nc.scalar.activation(k_hm[:, 0:P], k_first[:, 1, :].bitcast(f32), ACT.Copy).then_inc(k_first_copied, 1)
                eb, ej, e, there = head_at(b, j, h, 0)
                if there:
                    T, n = tile_of(eb, ej), (ej + 1) * P
                    need(act, biased, T * H + e + 1)
                    nc.scalar.activation(probs[:, e, 0:n], probs[:, e, 0:n], ACT.Exp, bias=neg_max[:, ej % 2, e:e + 1],
                                         scale=-1.0, accum_out=sums[:, ej % 2, e:e + 1]).then_inc(exp_done, 1)
                    if e % QUAD == QUAD - 1:
                        q = slice(e - QUAD + 1, e + 1)
                        need(act, null_d_done, T * QUAD + e // QUAD + 1)
                        nc.scalar.activation(null_e[:, ej % 2, q], null_d[:, ej % 2, q], ACT.Exp).then_inc(null_e_done, 1)

            run(act, step)

        @block.vector
        def _(dve):
            linked = [0]

            def link(ins):
                linked[0] += 1
                ins.then_inc(mlp_link, 1)
                dve.wait_ge(mlp_link, linked[0])

            dve.wait_ge(dma_small, 9 * 16)
            dve.wait_ge(zeroed, 1)
            link(nc.vector.memset(q_l1[DH:P].bitcast(f32), 1.0 / DH))
            for i in range(2):
                rows = slice(i * DH, (i + 1) * DH)
                flat = v_null_sel.rearrange("p a h -> p (a h)")
                link(nc.vector.tensor_copy(flat[rows, i:i + (PAIRS - 1) * (H + 2) + 1:H + 2], v_null[rows, :].to_broadcast([DH, PAIRS])))
            link(nc.vector.tensor_scalar(neg_null_bias[:], neg_null_bias[:], -1.0, None, ALU.mult))
            link(nc.vector.scalar_tensor_tensor(qk_scale[:], qk_tmp[:, 0, :], SCALE, qk_tmp[:, 1, :], ALU.mult, ALU.mult))
            nc.vector.tensor_tensor(k_null_sq, k_null, k_null, ALU.mult).then_inc(v_null_placed, 1)
            dve.wait_ge(v_null_placed, 1)
            link(nc.vector.tensor_reduce(norm2[:, 0, 0:1], k_null_sq, AX.X, ALU.add))
            nc.vector.tensor_scalar(norm2c[:, 0, 0:1], norm2[:, 0, 0:1], L2_EPS ** 2, None, ALU.max).then_inc(k_null_ve, 1)

            def layer_norm(layer):
                for t in range(NT):
                    link(nc.vector.bn_stats(s_st[:, t, :], mlp_h[:, t, :]))
                    link(nc.vector.bn_aggr(s_mv[:, t, :], s_st[:, t, :]))
                nc.vector.tensor_scalar(s_ve[:], s_mv[:, :, 1], LN_EPS, None, ALU.add).then_inc(mlp_ve, 1)
                dve.wait_ge(mlp_rs, layer + 1)
                for t in range(NT):
                    link(nc.vector.tensor_scalar(mlp_h[:, t, :], mlp_h[:, t, :], s_mv[:, t, 0:1], s_rs[:, t:t + 1], ALU.subtract, ALU.mult))
                    nc.vector.tensor_tensor(mlp_h[:, t, :], mlp_h[:, t, :], mlp_g[layer], ALU.mult).then_inc(mlp_affine, 1)
                for t in range(NT):
                    dve.wait_ge(mlp_tanh, NT * layer + t + 1)
                    nc.vector.scalar_tensor_tensor(mlp_h[:, t, :], tanh[(t + layer) % 3], 1.0, mlp_h[:, t, :], ALU.add, ALU.mult).then_inc(mlp_silu, 1)

            dve.wait_ge(dma_mlp, 7 * 16)
            dve.wait_ge(pos_made, 1)
            for t in range(NT):
                link(nc.vector.scalar_tensor_tensor(mlp_h[:, t, :], mlp_w0, pos[:, t:t + 1], mlp_b[0], ALU.mult, ALU.add))
            layer_norm(0)
            dve.wait_ge(k_null_rs, 1)
            link(nc.vector.scalar_tensor_tensor(k_null, k_null, rnorm[:, 0, 0:1], qk_scale[:], ALU.mult, ALU.mult))
            dve.wait_ge(dma_wq, 16)
            for c in range(DC):
                both = q_raw[:].rearrange("p (h d) -> p h d", d=DH)
                link(nc.vector.tensor_tensor(both, wq_stage[:, c, :].rearrange("p (h d) -> p h d", d=DH),
                                             k_null.unsqueeze(1).to_broadcast([P, H, DH]), ALU.mult))
                nc.vector.tensor_reduce(wkv_f[:, c, 2 * DH:KVN], both, AX.X, ALU.add).then_inc(wk_null, 1)
                dve.wait_ge(wk_null, c + 1)
                dve.wait_ge(wqh_made, c + 1)
                last = nc.vector.scalar_tensor_tensor(wq_l[:, c, :], wq_stage[:, c, :], g_norm_c[:, c:c + 1], wq_h[:, c, :], ALU.mult, ALU.subtract)
            last.then_inc(dve_staged, 1)
            dve.wait_ge(null_w_hi, 2)
            lo_half(nc.vector, null_w_tmp, psum[7][0:H, :], null_w[0:H, :]).then_inc(null_w_lo, 1)
            for t in range(NT):
                dve.wait_ge(h2_made, t + 1)
                link(nc.vector.tensor_tensor(mlp_h[:, t, :], psum[t][:], mlp_b[1], ALU.add))
            layer_norm(1)
            dve.wait_ge(woh_made, 1)
            lo_half(nc.vector, wo_l[:].rearrange("p c n -> p (c n)"), wout_stage.rearrange("p c n -> p (c n)"),
                    wo_h[:].rearrange("p c n -> p (c n)")).then_inc(dve_staged, 1)
            dve.wait_ge(table_made, 1)
            nc.vector.memset(table[:, S:TW], MASKED).then_inc(table_tail, 1)
            nc.vector.tensor_scalar(table[:, 0:S], psum[0][0:H, :], b2_c[:], None, ALU.add).then_inc(table_ready, 1)
            dve.wait_ge(wkh_made, DC)
            for c in range(DC):
                last = nc.vector.scalar_tensor_tensor(wk_l[:, c, :], wkv_f[:, c, :], g_norm_c[:, c:c + 1], wk_h[:, c, :], ALU.mult, ALU.subtract)
            last.then_inc(dve_staged, 1)
            for h in range(1, H, 2):
                dve.wait_ge(flipped, h + 1)
                nc.vector.tensor_copy(bias[:, h, :], psum[h % 8][:]).then_inc(bias_odd, 1)


            def step(b, j, h):
                up, (ub, uj) = real(b, j, 1), where(b, j, 1)
                U = tile_of(ub, uj)
                if up and h == X_AT + 1:
                    need(dve, xTh_ready, U + 1)
                    lo_half(nc.vector, xT_l[:].rearrange("p c n -> p (c n)"), m1[:], xT_h[:].rearrange("p c n -> p (c n)")).then_inc(xTl_ready, 1)
                for i in range(4):
                    off = QT_TILE[i] - (QT_AT[i] + 1) // H
                    if h == (QT_AT[i] + 1) % H and real(b, j, off):
                        V = tile_of(*where(b, j, off))
                        need(dve, qTh_ready, 4 * V + i + 1)
                        lo_half(nc.vector, q_l1[0:DH, 4 * i:4 * i + 4, :].rearrange("p c n -> p (c n)"), m0[0:DH, :],
                                q_hh[0:DH, 4 * i:4 * i + 4, :].rearrange("p c n -> p (c n)")).then_inc(qTl_ready, 1)
                ob, oj, hh, there = head_at(b, j, h, LAG_V + 1)
                if there and hh % QUAD == QUAD - 1:
                    O, g = tile_of(ob, oj), hh // QUAD
                    need(dve, oTh_ready, 4 * O + g + 1)
                    lo_half(nc.vector, oT_l[:, 2 * g:2 * g + 2, :].rearrange("p c n -> p (c n)"), o_bank[:, 0:2 * P],
                            oT_h[:, 2 * g:2 * g + 2, :].rearrange("p c n -> p (c n)")).then_inc(oTl_ready, 1)
                bb, jj, hh, there = head_at(b, j, h, LAG_T)
                if there and hh % 2:
                    T = tile_of(bb, jj)
                    need(dve, pT_made, T * H + hh + 1)
                    need(dve, pv_made, T * 4 + hh // QUAD)
                    n = (jj + 1) * P
                    nc.vector.tensor_copy(probs[:, TR + hh % PR, 0:n], pT_bank[1][:, 0:n]).then_inc(pT_odd, 1)
                for half, bank in ((0, m1), (1, m0)):
                    if up and h == Q_DONE[half] + 1:
                        need(dve, q_sq[half], U + 1)
                        nc.vector.tensor_reduce(norm2[:, uj % 2, half * 8:half * 8 + 8],
                                                bank[:].rearrange("p (a d) -> p a d", d=DH),
                                                AX.X, ALU.add).then_inc(norm2_done[half], 1)
                        need(dve, norm2_done[half], U + 1)
                        nc.vector.tensor_scalar(norm2c[:, uj % 2, half * 8:half * 8 + 8], norm2[:, uj % 2, half * 8:half * 8 + 8],
                                                L2_EPS ** 2, None, ALU.max).then_inc(norm2c_done, 1)
                if up and h == KV_AT + 2:
                    need(dve, k_sq, U + 1)
                    nc.vector.tensor_scalar(norm2c[:, uj % 2, H:H + 1], norm2[:, uj % 2, H:H + 1], L2_EPS ** 2, None, ALU.max).then_inc(k_norm2c_done, 1)
                if up and h == KV_AT + 5:
                    need(dve, k_rnorm_done, U + 1)
                    need(dve, kT_made, U)
                    need(dve, kv_copied, U + 1)
                    nc.vector.scalar_tensor_tensor(k_norm[:], kv[:, uj % 2, 0:DH].unsqueeze(1).to_broadcast([P, 2, DH]),
                                                   rnorm[:, uj % 2, H:H + 1], qk_scale[:].unsqueeze(1).to_broadcast([P, 2, DH]),
                                                   ALU.mult, ALU.mult).then_inc(k_norm_done, 1)
                if real(b, j, -1) and h == NULL_AT + 1:
                    ob, oj = where(b, j, -1)
                    need(dve, null_pT_hi, tile_of(ob, oj) + 1)
                    if up:
                        need(dve, kv_copied, U + 1)
                    lo_half(nc.vector, null_pT[32:64, :], m1[32:64, 2 * P:3 * P], null_pT[32:64, :]).then_inc(null_pT_ready, 1)
                if up and h == KT_AT + 1:
                    hl, hm = new_keys(uj)
                    need(dve, kTh_ready, U + 1)
                    lo_half(nc.vector, hl[DH:P, :], m0[DH:P, 0:P], hm[DH:P, :]).then_inc(k_hl_lo, 1)
                    need(dve, mask_loaded, 16 * (ub + 1))
                    need(dve, k_hl_lo, U + 1)
                    nc.vector.tensor_scalar(hm[DH:P, :], mask_u8[DH:P, uj * P:(uj + 1) * P], 1.0, -MASKED, ALU.subtract, ALU.mult).then_inc(kTl_ready, 1)
                for i in range(4):
                    if h == NORM_AT[i] and real(b, j, NORM_TILE[i]):
                        vb, vj = where(b, j, NORM_TILE[i])
                        V = tile_of(vb, vj)
                        need(dve, rnorm_done, 2 * V + i // 2 + 1)
                        need(dve, qT_made, 4 * V + i - 1)
                        slot = slice(4 * (i % 2), 4 * (i % 2) + 4)
                        nc.vector.tensor_tensor(q_norm[:, slot, 0, :], q_raw[:, 4 * i * DH:4 * (i + 1) * DH].rearrange("p (a d) -> p a d", d=DH),
                                                rnorm[:, vj % 2, 4 * i:4 * i + 4].unsqueeze(2).to_broadcast([P, 4, DH]), ALU.mult).then_inc(q_norm_done, 1)
                if real(b, j, 2):
                    lb, lj = where(b, j, 2)
                    L = tile_of(lb, lj)
                    if h == STATS_AT:
                        need(dve, x_loaded[lj], 16 * (lb + 1))
                        nc.vector.bn_stats(x_st[:], x_in[:, lj, :]).then_inc(x_st_done, 1)
                        need_apart(dve, x_st_done, L + 1)
                        nc.vector.bn_aggr(x_mv[:], x_st[:]).then_inc(x_mv_done, 1)
                        need(dve, x_mv_done, L + 1)
                        nc.vector.tensor_scalar(x_ve[:], x_mv[:, 1:2], LN_EPS, None, ALU.add).then_inc(x_ve_done, 1)
                    if h == X_NORM_AT:
                        need(dve, x_rs_done, L + 1)
                        need(dve, xT_made, L)
                        nc.vector.tensor_scalar(x_norm[:], x_in[:, lj, :], x_mv[:, 0:1], x_rs[:], ALU.subtract, ALU.mult).then_inc(x_norm_done, 1)
                ob, oj = where(b, j, -1)
                O = tile_of(ob, oj)
                if real(b, j, -1) and h == FINISH_AT:
                    need(dve, out_made, O + 1)
                    nc.vector.bn_stats(o_st[:], m1[:]).then_inc(o_st_done, 1)
                    need_apart(dve, o_st_done, O + 1)
                    nc.vector.bn_aggr(o_mv[:], o_st[:]).then_inc(o_mv_done, 1)
                    need(dve, o_mv_done, O + 1)
                    nc.vector.tensor_scalar(o_ve[:], o_mv[:, 1:2], LN_EPS, None, ALU.add).then_inc(o_ve_done, 1)
                if real(b, j, -1) and h == Z_AT:
                    need(dve, y_stored[oj % 2], 16 * (ob * (NT // 2) + oj // 2))
                    nc.vector.scalar_tensor_tensor(y[:, oj % 2, :], m1[:], o_mv[:, 0:1], g_out_b[:], ALU.subtract, ALU.mult).then_inc(z_done, 1)
                if real(b, j):
                    T, n = tile_of(b, j), (j + 1) * P
                    if h == 0:
                        need(dve, neg_null_s_done, T + 1)
                    need(dve, scores_made, T * H + h + 1)
                    need_apart(dve, pT_made, (T - 1) * H + h + 1)
                    nc.vector.tensor_tensor_reduce(out=probs[:, h, 0:n], in0=score_bank[(j * H + h) % SR][:, 0:n],
                                                   in1=bias[:, h, S - n:S], scale=-1.0,
                                                   scalar=neg_null_s[:, j % 2, h:h + 1], op0=ALU.add, op1=ALU.min,
                                                   accum_out=neg_max[:, j % 2, h:h + 1]).then_inc(biased, 1)
                    if h % QUAD == QUAD - 1:
                        q = slice(h - QUAD + 1, h + 1)
                        need(dve, biased, T * H + h + 1)
                        nc.vector.tensor_tensor(null_d[:, j % 2, q], neg_max[:, j % 2, q], neg_null_s[:, j % 2, q], ALU.subtract).then_inc(null_d_done, 1)
                qb, qj, qh, there = head_at(b, j, h, 1)
                if there and h % QUAD == 0:
                    Q = tile_of(qb, qj) * 4 + qh // QUAD
                    q = slice(qh - QUAD + 1, qh + 1)
                    need(dve, null_e_done, Q + 1)
                    nc.vector.tensor_tensor(den[:, qj % 2, q], sums[:, qj % 2, q], null_e[:, qj % 2, q], ALU.add).then_inc(den_done, 1)
                    need(dve, den_done, Q + 1)
                    nc.vector.reciprocal(rden[:, qj % 2, q], den[:, qj % 2, q]).then_inc(rden_done, 1)
                at_end = isinstance(b, int) and tile_of(b, j) == TILES and h == H - 1
                if at_end or (h == Y_AT % H and real(b, j, -1 - Y_AT // H)):
                    ob, oj = (B - 1, NT - 1) if at_end else where(b, j, -1 - Y_AT // H)
                    O = tile_of(ob, oj)
                    need(dve, z_done, O + 1)
                    need(dve, o_rs_done, O + 1)
                    nc.vector.scalar_tensor_tensor(y[:, oj % 2, :], y[:, oj % 2, :], o_rs[:], x_in[:, oj, :], ALU.mult, ALU.add).then_inc(y_done, 1)

            run(dve, step)

        @block.gpsimd
        def _(pool):
            nc.gpsimd.memset(v_null_sel, 0.0).then_inc(zeroed, 1)
            nc.gpsimd.memset(ident[:], 0.0).then_inc(zeroed, 1)
            nc.gpsimd.memset(flip[:], 0.0).then_inc(zeroed, 1)
            nc.gpsimd.memset(neg_half[:], -0.5).then_inc(zeroed, 1)
            nc.gpsimd.memset(null_p[:], 0.0).then_inc(zeroed, 1)
            nc.gpsimd.memset(null_w[:].bitcast(f32), 0.0).then_inc(zeroed, 1)
            nc.gpsimd.iota(pos[:], pattern=[[-P, NT]], base=S - 1, channel_multiplier=-1,
                           allow_small_or_imprecise_dtypes=True).then_inc(pos_made, 1)
            pool.wait_ge(zeroed, 6)
            nc.gpsimd.affine_select(out=ident[:], in_=ident[:], compare_op=ALU.not_equal, fill=1.0, base=0,
                                    pattern=[[-1, P]], channel_multiplier=1).then_inc(ident_made, 1)
            nc.gpsimd.affine_select(out=flip[:], in_=flip[:], compare_op=ALU.not_equal, fill=1.0, base=1 - P,
                                    pattern=[[1, P]], channel_multiplier=1).then_inc(ident_made, 1)
            pool.wait_ge(k_null_ve, 1)
            nc.gpsimd.tensor_tensor(rnorm[:, 0, 0:1], norm2c[:, 0, 0:1], neg_half[:, 0:1], ALU.pow).then_inc(k_null_rs, 1)
            for layer in range(2):
                pool.wait_ge(mlp_ve, layer + 1)
                nc.gpsimd.tensor_tensor(s_rs[:], s_ve[:], neg_half[:, 0:NT], ALU.pow).then_inc(mlp_rs, 1)


            def step(b, j, h):
                up, (ub, uj) = real(b, j, 1), where(b, j, 1)
                U = tile_of(ub, uj)
                for half in range(2):
                    if up and h == Q_DONE[half] + 2:
                        part = slice(half * 8, half * 8 + 8)
                        need(pool, norm2c_done, 2 * U + half + 1)
                        nc.gpsimd.tensor_tensor(rnorm[:, uj % 2, part], norm2c[:, uj % 2, part], neg_half[:, 0:8], ALU.pow).then_inc(rnorm_done, 1)
                qb, qj, qh, there = head_at(b, j, h, 1)
                if there and h % QUAD == 0:
                    T, n = tile_of(qb, qj), (qj + 1) * P
                    need(pool, rden_done, T * 4 + qh // QUAD + 1)
                    q = slice(qh - 3, qh + 1)
                    need(pool, null_pT_made, T - 1)
                    nc.gpsimd.tensor_tensor(null_p[:, qj % 2, :, q], null_e[:, qj % 2, q].unsqueeze(1).to_broadcast([P, 3, QUAD]),
                                            rden[:, qj % 2, q].unsqueeze(1).to_broadcast([P, 3, QUAD]), ALU.mult).then_inc(null_p_done, 1)
                    for lo in (qh - 3, qh - 1):
                        nc.gpsimd.tensor_tensor(probs[:, lo:lo + 2, 0:n], probs[:, lo:lo + 2, 0:n],
                                                rden[:, qj % 2, lo:lo + 2].unsqueeze(2).to_broadcast([P, 2, n]), ALU.mult).then_inc(scaled, 1)
                for i in range(4):
                    if h == NORM_AT[i] and real(b, j, NORM_TILE[i]):
                        vb, vj = where(b, j, NORM_TILE[i])
                        V = tile_of(vb, vj)
                        need(pool, rnorm_done, 2 * V + i // 2 + 1)
                        need(pool, qT_made, 4 * V + i - 1)
                        slot = slice(4 * (i % 2), 4 * (i % 2) + 4)
                        nc.gpsimd.tensor_tensor(q_norm[:, slot, 1, :], q_raw[:, 4 * i * DH:4 * (i + 1) * DH].rearrange("p (a d) -> p a d", d=DH),
                                                rnorm[:, vj % 2, 4 * i:4 * i + 4].unsqueeze(2).to_broadcast([P, 4, DH]), ALU.mult).then_inc(q_norm_twice, 1)
                if up and h == KV_AT + 2:
                    need(pool, k_norm2c_done, U + 1)
                    nc.gpsimd.tensor_tensor(rnorm[:, uj % 2, H:H + 1], norm2c[:, uj % 2, H:H + 1], neg_half[:, 0:1], ALU.pow).then_inc(k_rnorm_done, 1)
                if real(b, j) and h == (3 if j else 10):
                    T = tile_of(b, j)
                    if j == 0:
                        need(pool, pv_made, T * 4)
                    need_apart(pool, kv_copied, T + 1)
                    nc.gpsimd.tensor_copy(v[:, j, :], kv[:, j % 2, DH:2 * DH]).then_inc(v_copied, 1)
                if up and h == Q_DONE[1] + 2:
                    need(pool, kv_copied, U + 1)
                    need(pool, rnorm_done, 2 * U + 2)
                    nc.gpsimd.tensor_tensor(null_s[:], kv[:, uj % 2, 2 * DH:KVN], rnorm[:, uj % 2, 0:H], ALU.mult).then_inc(null_s_done, 1)
                    need(pool, null_s_done, U + 1)
                    nc.gpsimd.tensor_tensor(neg_null_s[:, uj % 2, :], neg_null_bias[:], null_s[:], ALU.subtract).then_inc(neg_null_s_done, 1)
                if real(b, j, 2) and h == STATS_AT + 1:
                    lb, lj = where(b, j, 2)
                    need(pool, x_ve_done, tile_of(lb, lj) + 1)
                    nc.gpsimd.tensor_tensor(x_rs[:], x_ve[:], neg_half[:, 0:1], ALU.pow).then_inc(x_rs_done, 1)
                if real(b, j, -1) and h == FINISH_AT:
                    ob, oj = where(b, j, -1)
                    need(pool, o_ve_done, tile_of(ob, oj) + 1)
                    nc.gpsimd.tensor_tensor(o_rs[:], o_ve[:], neg_half[:, 0:1], ALU.pow).then_inc(o_rs_done, 1)

            run(pool, step)


_INS = ['x', 'cond_64', 'mask_BxS_bf1', 'L0_cond_g_norm', 'L0_cond_Wq', 'L0_cond_Wkv', 'L0_cond_q_scale',
        'L0_cond_k_scale', 'L0_cond_null_attn_bias', 'L0_cond_w0', 'L0_cond_b0', 'L0_cond_g0', 'L0_cond_w1',
        'L0_cond_b1', 'L0_cond_g1', 'L0_cond_w2', 'L0_cond_b2', 'L0_cond_Wout', 'L0_cond_g_out']


def kernel(**inputs):
    import numpy as np
    import concourse.bacc as bacc
    from concourse.bass_utils import run_bass_kernel_spmd

    nc = bacc.Bacc("TRN2", target_bir_lowering=False, num_devices=1)
    arrays, args = {}, []
    for name in _INS:
        a = np.ascontiguousarray(inputs[name])
        if a.dtype == np.bool_:
            a = a.view(np.uint8)
        arrays[f"in_{name}"] = a
        args.append(nc.dram_tensor(f"in_{name}", a.shape, mybir.dt.from_np(a.dtype), kind="ExternalInput").ap())
    S, H = inputs['x'].shape[1], inputs['L0_cond_null_attn_bias'].shape[0]
    args.append(nc.dram_tensor("bias_table", (H, S + 128), mybir.dt.float32, kind="Internal").ap())
    args.append(nc.dram_tensor("out", inputs['x'].shape, mybir.dt.float32, kind="ExternalOutput").ap())
    cond_attention_kernel(nc, *args)
    r = run_bass_kernel_spmd(nc, [arrays], core_ids=[0])
    return r.results[0]["out"]
```
